# Optimizing a Trainium2 kernel written in Bass

```python
import numpy as np
import jax
import jax.numpy as jnp

def _softmax(x, axis=-1):
    return jax.nn.softmax(x, axis=axis)

def _gelu(x):
    return jax.nn.gelu(x, approximate=True)

def _silu(x):
    return jax.nn.silu(x)

def _sigmoid(x):
    return jax.nn.sigmoid(x)

def _layernorm(x, axis=-1, eps=1e-05):
    m = jnp.mean(x, axis=axis, keepdims=True)
    v = jnp.var(x, axis=axis, keepdims=True)
    return (x - m) / jnp.sqrt(v + eps)

def _scatter_add(tgt, idx, src, axis=0):
    return tgt.at[idx].add(src)

def _segment_sum(src, seg, n):
    return jax.ops.segment_sum(src, seg, n)
kernel_name = 'mk_prb_d1_jaxref_r8_192365'

def setup_inputs(seed: int=0):
    np.random.seed(seed)
    _w = jnp.asarray

    def _L0_attn_setup():
        import jax, jax.numpy as jnp
        import numpy as np
        import math
        D_MODEL, D_C, D_R, NH = (128, 128, 32, 16)
        HD = D_MODEL // NH
        B, T = (2, 256)

        def _rope_tables(T, d_R):
            inv_freq = 1.0 / 10000.0 ** (jnp.arange(0, d_R, 2, dtype=jnp.float32) / d_R)
            t = jnp.arange(T, dtype=jnp.float32)
            freqs = jnp.outer(t, inv_freq)
            return (jnp.cos(freqs), jnp.sin(freqs))

        def _rotary_apply(x, cos, sin):
            d = x.shape[-1]
            x1, x2 = (x[..., :d // 2], x[..., d // 2:])
            return jnp.concatenate([x1 * cos - x2 * sin, x2 * cos + x1 * sin], axis=-1)
        key = jax.random.key(seed)
        ks = jax.random.split(key, 8)
        s = lambda fan_in: 1.0 / math.sqrt(fan_in)
        return {'x': jax.random.normal(ks[0], (B, T, D_MODEL), jnp.float32), 'W_kv_down': jax.random.normal(ks[1], (D_MODEL, D_C), jnp.float32) * s(D_MODEL), 'W_k_up': jax.random.normal(ks[2], (D_C, D_MODEL), jnp.float32) * s(D_C), 'W_v_up': jax.random.normal(ks[3], (D_C, D_MODEL), jnp.float32) * s(D_C), 'W_q': jax.random.normal(ks[4], (D_MODEL, D_MODEL), jnp.float32) * s(D_MODEL), 'W_q_rope': jax.random.normal(ks[5], (D_MODEL, D_R), jnp.float32) * s(D_MODEL), 'W_k_rope': jax.random.normal(ks[6], (D_C, D_R), jnp.float32) * s(D_C), 'W_o': jax.random.normal(ks[7], (D_MODEL, D_MODEL), jnp.float32) * s(D_MODEL)}
    _L0_attn_in = _L0_attn_setup()

    def _L0_ffn_setup():
        import jax, jax.numpy as jnp
        import numpy as np
        B, S, H, DFF, E, K = (2, 256, 128, 256, 8, 2)

        def _moe(x, Wg, W1, b1, W2, b2, W3, b3):
            Bm, Sm, Hm = x.shape
            xt = x.reshape(-1, Hm)
            gout = xt @ Wg.T
            topv, topi = jax.lax.top_k(gout, K)
            w = jax.nn.softmax(topv, axis=-1)
            comb = jnp.einsum('tke,tk->te', jax.nn.one_hot(topi, E, dtype=x.dtype), w)
            g = jnp.einsum('th,efh->etf', xt, W1) + b1[:, None, :]
            v = jnp.einsum('th,efh->etf', xt, W2) + b2[:, None, :]
            h = jax.nn.silu(g) * v
            eo = jnp.einsum('etf,ehf->eth', h, W3) + b3[:, None, :]
            out = jnp.einsum('eth,te->th', eo, comb)
            return out.reshape(Bm, Sm, Hm)
        key = jax.random.key(seed)
        ks = jax.random.split(key, 8)
        sc_h = 1.0 / np.sqrt(H)
        sc_f = 1.0 / np.sqrt(DFF)
        x = jax.random.normal(ks[0], (B, S, H), dtype=jnp.float32)
        Wg = jax.random.uniform(ks[1], (E, H), jnp.float32, -sc_h, sc_h)
        W1 = jax.random.uniform(ks[2], (E, DFF, H), jnp.float32, -sc_h, sc_h)
        b1 = jax.random.uniform(ks[3], (E, DFF), jnp.float32, -sc_h, sc_h)
        W2 = jax.random.uniform(ks[4], (E, DFF, H), jnp.float32, -sc_h, sc_h)
        b2 = jax.random.uniform(ks[5], (E, DFF), jnp.float32, -sc_h, sc_h)
        W3 = jax.random.uniform(ks[6], (E, H, DFF), jnp.float32, -sc_f, sc_f)
        b3 = jax.random.uniform(ks[7], (E, H), jnp.float32, -sc_f, sc_f)
        return {'x': x, 'Wg': Wg, 'W1': W1, 'b1': b1, 'W2': W2, 'b2': b2, 'W3': W3, 'b3': b3}
    _L0_ffn_in = _L0_ffn_setup()
    _d = {'L0_attn_x': _L0_attn_in['x'], 'L0_attn_W_kv_down': _L0_attn_in['W_kv_down'], 'L0_attn_W_k_up': _L0_attn_in['W_k_up'], 'L0_attn_W_v_up': _L0_attn_in['W_v_up'], 'L0_attn_W_q': _L0_attn_in['W_q'], 'L0_attn_W_q_rope': _L0_attn_in['W_q_rope'], 'L0_attn_W_k_rope': _L0_attn_in['W_k_rope'], 'L0_attn_W_o': _L0_attn_in['W_o'], 'L0_ffn_Wg': _L0_ffn_in['Wg'], 'L0_ffn_W1': _L0_ffn_in['W1'], 'L0_ffn_b1': _L0_ffn_in['b1'], 'L0_ffn_W2': _L0_ffn_in['W2'], 'L0_ffn_b2': _L0_ffn_in['b2'], 'L0_ffn_W3': _L0_ffn_in['W3'], 'L0_ffn_b3': _L0_ffn_in['b3']}
    _x0 = _d['L0_attn_x']
    _d['L0_attn_x'] = jax.random.normal(jax.random.fold_in(jax.random.key(seed), 1), (2, 1024, 128), dtype=_x0.dtype)
    del _x0
    return _d

def reference(L0_attn_x, L0_attn_W_kv_down, L0_attn_W_k_up, L0_attn_W_v_up, L0_attn_W_q, L0_attn_W_q_rope, L0_attn_W_k_rope, L0_attn_W_o, L0_ffn_Wg, L0_ffn_W1, L0_ffn_b1, L0_ffn_W2, L0_ffn_b2, L0_ffn_W3, L0_ffn_b3):

    def _L0_attn_ref(x, W_kv_down, W_k_up, W_v_up, W_q, W_q_rope, W_k_rope, W_o):
        import jax, jax.numpy as jnp
        import numpy as np
        import math
        D_MODEL, D_C, D_R, NH = (128, 128, 32, 16)
        HD = D_MODEL // NH
        B, T = (2, 256)

        def _rope_tables(T, d_R):
            inv_freq = 1.0 / 10000.0 ** (jnp.arange(0, d_R, 2, dtype=jnp.float32) / d_R)
            t = jnp.arange(T, dtype=jnp.float32)
            freqs = jnp.outer(t, inv_freq)
            return (jnp.cos(freqs), jnp.sin(freqs))

        def _rotary_apply(x, cos, sin):
            d = x.shape[-1]
            x1, x2 = (x[..., :d // 2], x[..., d // 2:])
            return jnp.concatenate([x1 * cos - x2 * sin, x2 * cos + x1 * sin], axis=-1)
        Bb, Tt, _ = x.shape
        cos, sin = _rope_tables(Tt, D_R)
        cos = cos[None]
        sin = sin[None]
        c_kv = x @ W_kv_down
        k_rope = _rotary_apply(c_kv @ W_k_rope, cos, sin)
        k = (c_kv @ W_k_up).reshape(Bb, Tt, NH, HD)
        v = (c_kv @ W_v_up).reshape(Bb, Tt, NH, HD)
        q = (x @ W_q).reshape(Bb, Tt, NH, HD)
        q_rope = _rotary_apply(x @ W_q_rope, cos, sin)
        scale = math.sqrt(HD + D_R)
        scores = jnp.einsum('bqhd,bkhd->bhqk', q, k)
        scores = scores + jnp.einsum('bqr,bkr->bqk', q_rope, k_rope)[:, None]
        scores = scores / scale
        causal = jnp.triu(jnp.ones((Tt, Tt), dtype=bool), k=1)
        scores = jnp.where(causal[None, None], -jnp.inf, scores)
        w = jax.nn.softmax(scores, axis=-1)
        attn = jnp.einsum('bhqk,bkhd->bqhd', w, v).reshape(Bb, Tt, D_MODEL)
        return attn @ W_o

    def _L0_ffn_ref(x, Wg, W1, b1, W2, b2, W3, b3):
        import jax, jax.numpy as jnp
        import numpy as np
        B, S, H, DFF, E, K = (2, 256, 128, 256, 8, 2)

        def _moe(x, Wg, W1, b1, W2, b2, W3, b3):
            Bm, Sm, Hm = x.shape
            xt = x.reshape(-1, Hm)
            gout = xt @ Wg.T
            topv, topi = jax.lax.top_k(gout, K)
            w = jax.nn.softmax(topv, axis=-1)
            comb = jnp.einsum('tke,tk->te', jax.nn.one_hot(topi, E, dtype=x.dtype), w)
            g = jnp.einsum('th,efh->etf', xt, W1) + b1[:, None, :]
            v = jnp.einsum('th,efh->etf', xt, W2) + b2[:, None, :]
            h = jax.nn.silu(g) * v
            eo = jnp.einsum('etf,ehf->eth', h, W3) + b3[:, None, :]
            out = jnp.einsum('eth,te->th', eo, comb)
            return out.reshape(Bm, Sm, Hm)
        return _moe(x, Wg, W1, b1, W2, b2, W3, b3)
    x = L0_attn_x
    xn = _layernorm(x, axis=-1)
    x = x + _L0_attn_ref(xn, L0_attn_W_kv_down, L0_attn_W_k_up, L0_attn_W_v_up, L0_attn_W_q, L0_attn_W_q_rope, L0_attn_W_k_rope, L0_attn_W_o) + _L0_ffn_ref(xn, L0_ffn_Wg, L0_ffn_W1, L0_ffn_b1, L0_ffn_W2, L0_ffn_b2, L0_ffn_W3, L0_ffn_b3)
    return x

_drawn_inputs = setup_inputs


def setup_inputs(seed=0):
    import zlib

    import numpy as np

    out = dict(_drawn_inputs(seed))
    spreads = {}
    factors = {'L0_ffn_b1': 8.0, 'L0_ffn_b2': 8.0}
    for name, (base, spread) in spreads.items():
        noise = np.random.default_rng([zlib.crc32(name.encode()), seed]).standard_normal(out[name].shape)
        drawn = base * np.exp(spread * noise) if base else spread * noise
        out[name] = jnp.asarray(drawn.astype(out[name].dtype))
    for name, factor in factors.items():
        out[name] = (out[name] * factor).astype(out[name].dtype)
    return out
```

```python
from contextlib import ExitStack

import numpy as np
import concourse.bass as bass
from concourse import mybir

F32 = mybir.dt.float32
F16 = mybir.dt.float16
BF16 = mybir.dt.bfloat16
I32 = mybir.dt.int32
U32 = mybir.dt.uint32
ALU = mybir.AluOpType
ACT = mybir.ActivationFunctionType
AX = mybir.AxisListType

PART = 128
BANK = 512
B, T, D = 2, 1024, 128
NH, HD, DR = 16, 8, 32
E, FF = 8, 256
TOK = B * T
NT = TOK // PART
NC = TOK // BANK
TPC = BANK // PART
FJ = FF // PART
G4 = 4
GPB = NH // G4
NG = B * GPB
KT = T // PART
CPB = T // BANK
EPS = 1e-5
KAPPA = 2.0 ** 15
NEG = -1e30
HROW, RROW = 3 * HD, 3 * DR
QK_ROWS = HROW + RROW
ALL_ROWS = QK_ROWS + 2

PACK = {}
_at = 0
for _name, _n in (("wq", D), ("wqr", 2 * DR), ("wkv", D), ("wk", D), ("wkr", 2 * DR), ("wv", D), ("wo", D),
                  ("wg", E), ("b1", E * FJ), ("b2", E * FJ), ("iota", E)):
    PACK[_name] = (_at, _at + _n)
    _at += _n
PACK_COLS = _at

QLO, KHI, QHI, KLO = range(4)


def columns(g):
    out = []
    for c in range(CPB):
        for kt in range(TPC * (c + 1)):
            out.append((c, kt, max(0, kt * PART - c * BANK), kt >= c * TPC))
    return out


NCOL = len(columns(0))


def max_items(g):
    one = [("max1", g, j, i) for j in range(G4) for i in range(KT - 1, TPC - 1, -1)]
    two = [("max2", g, j, i) for j in range(0, G4, 2) for i in range(TPC)]
    return one + two


def schedule():
    stream = []
    for g in range(NG):
        items = max_items(g)
        if g:
            items.insert(2, ("mT", g - 1))
        stream += items
    stream.append(("mT", NG - 1))
    ahead = len(max_items(0)) + 1 + 12
    first, rest = stream[:ahead], stream[ahead:]
    slots = []
    total = (NG - 1) * NCOL - 4
    given = 0
    for n in range(NG * NCOL):
        want = min(len(rest), -(-len(rest) * (n + 1) // total))
        here = rest[given:want]
        given = want
        g, k = divmod(n, NCOL)
        if k == TPC + 1:
            here.append(("oT", g, 0))
        if k == 1 and g:
            here.append(("oT", g - 1, 1))
        if g % GPB == 0 and g and 2 <= k < 6:
            here.append((("aT", "wo")[k % 2], g // GPB - 1, (k - 2) // 2))
        slots.append(here)
    tail = [("oT", NG - 1, 1), ("aT", B - 1, 0), ("aT", B - 1, 1), ("wo", B - 1, 0), ("wo", B - 1, 1)]
    return first, slots, tail


def build(nc, x, wpack, w12, w3, b3, rope, out):
    first, slots, tail = schedule()
    ring_order = first + [i for s in slots for i in s] + tail
    ring_at = {item: r for r, item in enumerate(ring_order)}

    with ExitStack() as ctx:
        def sb(name, shape, dt, scope=ctx):
            return scope.enter_context(nc.sbuf_tensor(name, shape, dt))

        def sem(name):
            return ctx.enter_context(nc.semaphore(name))

        acc = sb("acc", [PART, NT, D], F32)
        x_t = sb("x_t", [D, TOK], F32)
        x_hi = sb("x_hi", [D, TOK], F16)
        x_lo = sb("x_lo", [D, TOK], F16)
        pack = sb("pack", [PART, PACK_COLS], F32)
        b3_sb = sb("b3_sb", [E, D], F32)
        identf = sb("identf", [PART, PART], F32)
        identh = sb("identh", [PART, PART], F16)
        identb = sb("identb", [PART, PART], BF16)
        causal = sb("causal", [PART, PART], BF16)
        v_aug = sb("v_aug", [PART, NT, NH, 32], F32)
        planes = sb("planes", [PART, 4, TOK], F16)
        rope_s = sb("rope_s", [PART, TOK], F16)
        kappa = sb("kappa", [2, T], F16)
        stack_a = sb("stack_a", [PART, G4, 2, T], F16)
        comb = sb("comb", [PART, NT, E], F32)
        comb_s = sb("comb_s", [PART, NT, E], F32)
        comb_t = sb("comb_t", [E, TOK], F32)
        attn = sb("attn", [PART, B, KT, D], F32)
        attn_t = sb("attn_t", [D, 2, BANK], F32)
        o_sb = sb("o_sb", [PART, 2, BANK], F32)
        rden = sb("rden", [PART, 2, TPC, G4], F32)
        maxima = sb("maxima", [PART, 2, G4, KT], F32)
        max_s = sb("max_s", [PART, 2, 2, G4, KT], F16)
        max_t = sb("max_t", [2 * G4 * KT, 2, PART], F16)
        amax = sb("amax", [PART, 8], F32)
        amax_all = sb("amax_all", [PART, 8], F32)
        pow2 = sb("pow2", [PART, 8], F32)
        ipow = sb("ipow", [PART, 8], F32)
        scales = sb("scales", [PART, 10], F32)
        ALPHA, BETA, GAMMA, A1, IA1, A2, IA2, TMP = (scales[:, i:i + 1] for i in range(8))
        b1_e = sb("b1_e", [PART, FJ], F32)
        b2_s = sb("b2_s", [PART, E * FJ], F32)

        early = ExitStack()
        raw12 = sb("raw12", [D, 2, E * FF], F32, early)
        w_hi = sb("w_hi", [D, 2, E * FF], F16, early)
        w_lo = sb("w_lo", [D, 2, E * FF], F16, early)
        w3_sb = sb("w3_sb", [PART, E * FJ * D], F32, early)
        logit = sb("logit", [PART, NT, E], F32, early)
        top = sb("top", [PART, NT, 8], F32, early)
        topi = sb("topi", [PART, NT, 8], U32, early)
        topf = sb("topf", [PART, NT, 8], F32, early)
        rw = sb("rw", [PART, 4, NT], F32, early)
        eq = sb("eq", [PART, 2, NT, E], F32, early)
        front = ExitStack()
        xn = sb("xn", [PART, NT, D], F32, front)
        c_t = sb("c_t", [D, TOK], F32, front)
        rope_c = sb("rope_c", [PART, T], F32, front)
        rope_m = sb("rope_m", [PART, 2, BANK, 2], F32, front)
        stats = sb("stats", [PART, NT, 6], F32, front)
        mv = sb("mv", [PART, NT, 2], F32, front)
        ln = sb("ln", [PART, 6, NT], F32, front)
        front.close()
        hid = sb("hid", [PART, 2, FJ, BANK], F32, early)
        silu = sb("silu", [PART, 2, BANK], F32, early)
        early.close()
        late = ctx.enter_context(ExitStack())
        stack_b = sb("stack_b", [PART, NH - G4, 2, T], F16, late)
        probs = sb("probs", [PART, 3, G4, BANK], F32, late)

        ps = ctx.enter_context(nc.psum_tensor("ps", [PART, 8 * BANK], F32))

        def bank(n, a=0, b=BANK, p0=0, p1=PART):
            return ps[p0:p1, n * BANK + a:n * BANK + b]

        def w(name):
            return pack[:, PACK[name][0]:PACK[name][1]]

        def stack(slot, rows, part, a=0, b=T):
            if slot < G4:
                return stack_a[rows[0]:rows[1], slot, part, a:b]
            return stack_b[rows[0]:rows[1], slot - G4, part, a:b]

        def stacks(first_slot, rows, part):
            if first_slot < G4:
                return stack_a[rows[0]:rows[1], :, part, :]
            return stack_b[rows[0]:rows[1], first_slot - G4:first_slot, part, :]

        ld_x = [sem(f"ld_x{c}") for c in range(NC)]
        ld_pack, ld_w12, ld_w3, ld_b3, ld_rope = (sem(n) for n in ("ld_pack", "ld_w12", "ld_w3", "ld_b3", "ld_rope"))
        pool_const = sem("pool_const")
        amax_done = sem("amax_done")
        amax_red = sem("amax_red")
        dve_chain = sem("dve_chain")
        pool_chain = sem("pool_chain")
        scales_ready = sem("scales_ready")
        var_ready = sem("var_ready")
        sqrt_done = sem("sqrt_done")
        xn_ready = sem("xn_ready")
        xt_ready, xt_done, xhi_done, xlo_done = (sem(n) for n in ("xt_ready", "xt_done", "xhi_done", "xlo_done"))
        q_ready, qhi_done, qlo_done = (sem(n) for n in ("q_ready", "qhi_done", "qlo_done"))
        c_ready, ct_done = sem("c_ready"), sem("ct_done")
        r_ready, rmul_done, radd_done, rhi_done, rlo_done = (
            sem(n) for n in ("r_ready", "rmul_done", "radd_done", "rhi_done", "rlo_done"))
        k_ready, khi_done, klo_done = (sem(n) for n in ("k_ready", "khi_done", "klo_done"))
        v_ready, v_done = sem("v_ready"), sem("v_done")
        gate_ready, gap_ready, gexp_done, comb_ready = (
            sem(n) for n in ("gate_ready", "gap_ready", "gexp_done", "comb_ready"))
        combt_ready, combt_done = sem("combt_ready"), sem("combt_done")
        whi_done, wlo_done = sem("whi_done"), sem("wlo_done")
        up_g, up_v = sem("up_g"), sem("up_v")
        b1_done = sem("b1_done")
        silu_done = sem("silu_done")
        hid_done = sem("hid_done")
        down_ready = sem("down_ready")
        mix_done = sem("mix_done")
        load = [sem(f"load{g}") for g in range(NG)]
        mrow = [sem(f"mrow{g}") for g in range(NG)]
        ring_ready, ring_done = sem("ring_ready"), sem("ring_done")
        msplit_done = sem("msplit_done")
        s_ready, exp_done = sem("s_ready"), sem("exp_done")
        mask_done = sem("mask_done")
        pv_done = sem("pv_done")
        o_done = sem("o_done")
        out_sem = sem("out_sem")

        block = ctx.enter_context(nc.Block())
        gh = (0, 64)

        @block.sync
        def _(sp):
            xv = x.rearrange("(c t p) d -> c p t d", p=PART, t=TPC)
            for c in range(NC):
                sp.dma_start(acc[:, c * TPC:(c + 1) * TPC, :], xv[c]).then_inc(ld_x[c], 16)
            for i in range(2):
                sp.dma_start(raw12[:, i, :], w12[i]).then_inc(ld_w12, 16)
            sp.dma_start(w3_sb[:, :], w3).then_inc(ld_w3, 16)

            def load_group(g):
                b, slot0 = g // GPB, G4 * (g % GPB)
                cols = slice(b * T, (b + 1) * T)

                def rot(rows, part, src):
                    sp.dma_start(stacks(slot0, (HROW + rows[0] * DR, HROW + rows[1] * DR), part),
                                 rope_s[src[0]:src[1], cols].unsqueeze(1).broadcast_to([src[1] - src[0], G4, T])
                                 ).then_inc(load[g], 16)
                rot((0, 2), 0, (0, 64))
                rot((2, 3), 0, (0, 32))
                rot((0, 1), 1, (64, 96))
                rot((1, 3), 1, (64, 128))
                if b == 0:
                    sp.dma_start(stacks(slot0, (QK_ROWS, ALL_ROWS), 1),
                                 kappa[:, :].unsqueeze(1).broadcast_to([2, G4, T])).then_inc(load[g], 16)
                for j in range(G4):
                    h = (g % GPB) * G4 + j
                    src = slice(h * HD, (h + 1) * HD)
                    st = stack_a[:, slot0 + j] if slot0 == 0 else stack_b[:, slot0 - G4 + j]
                    sp.dma_start(st[0:HD, :, :], planes[src, QLO:KHI + 1, cols]).then_inc(load[g], 16)
                    sp.dma_start(st[HD:2 * HD, :, :], planes[src, QHI:KLO + 1, cols]).then_inc(load[g], 16)
                    sp.dma_start(st[2 * HD:3 * HD, 0, :], planes[src, QHI, cols]).then_inc(load[g], 16)
                    sp.dma_start(st[2 * HD:3 * HD, 1, :], planes[src, KHI, cols]).then_inc(load[g], 16)

            def store_maxima(g):
                sp.wait_ge(ring_done, ring_at["mT", g] + 1)
                slot0 = G4 * (g % GPB)
                for p in range(2):
                    for j in range(G4):
                        n = (p * G4 + j) * KT
                        sp.dma_start(stack(slot0 + j, (QK_ROWS + p, QK_ROWS + p + 1), 0),
                                     max_t[n:n + KT, g % 2, :]).then_inc(mrow[g], 16)

            sp.wait_ge(pool_const, 6)
            for s, n in ((qhi_done, NC), (qlo_done, NC), (khi_done, NC), (klo_done, NC)):
                sp.wait_ge(s, n)
            sp.wait_ge(rhi_done, 2 * NC)
            sp.wait_ge(rlo_done, 2 * NC)
            load_group(0)
            sp.wait_ge(hid_done, 2 + E * NC * FJ)
            sp.wait_ge(mix_done, 2 + E * NC)
            sp.wait_ge(comb_ready, 1)
            sp.wait_ge(combt_ready, 1)
            for g in range(1, GPB):
                load_group(g)
            store_maxima(0)
            store_maxima(1)
            for g in range(GPB, NG):
                sp.wait_ge(s_ready, G4 * NCOL * (g - GPB + 1))
                load_group(g)
                store_maxima(g - 2)
            store_maxima(NG - 2)
            store_maxima(NG - 1)
            ov = out.rearrange("(c t p) d -> c p t d", p=PART, t=TPC)
            for b in range(B):
                for c in range(CPB):
                    n = b * CPB + c
                    sp.wait_ge(ring_done, ring_at["wo", b, c] + 1)
                    sp.dma_start(ov[n], acc[:, n * TPC:(n + 1) * TPC, :]).then_inc(out_sem, 16)
            sp.wait_ge(out_sem, 16 * NC)

        @block.gpsimd
        def _(pool):
            pool.memset(identf[:, :], 0.0).then_inc(pool_chain, 1)
            pool.memset(causal[:, :], 0.0).then_inc(pool_chain, 1)
            pool.wait_ge(pool_chain, 1)
            pool.affine_select(out=identf[:, :], in_=identf[:, :], compare_op=ALU.not_equal, fill=1.0, base=0,
                               pattern=[[-1, PART]], channel_multiplier=1).then_inc(pool_const, 1)
            pool.wait_ge(pool_const, 1)
            pool.tensor_copy(identh[:, :], identf[:, :]).then_inc(pool_const, 1)
            pool.tensor_copy(identb[:, :], identf[:, :]).then_inc(pool_const, 1)
            pool.wait_ge(amax_done, 3)
            pool.partition_all_reduce(amax_all[:, 0:3], amax[:, 0:3], PART, bass.bass_isa.ReduceOp.max
                                      ).then_inc(amax_red, 1)
            pool.wait_ge(pool_chain, 2)
            pool.affine_select(out=causal[:, :], in_=causal[:, :], compare_op=ALU.is_ge, fill=NEG, base=0,
                               pattern=[[-1, PART]], channel_multiplier=1).then_inc(pool_const, 1)
            pool.memset(v_aug[:, :, :, :], 0.0).then_inc(pool_chain, 1)
            pool.wait_ge(pool_chain, 3)
            pool.memset(v_aug[:, :, :, HD:HD + 1], 1.0).then_inc(pool_const, 1)
            pool.memset(kappa[:, :], KAPPA).then_inc(pool_const, 1)
            for n in range(2 * NC):
                if n == NC:
                    pool.wait_ge(amax_done, 5)
                    pool.partition_all_reduce(amax_all[:, 3:5], amax[:, 3:5], PART, bass.bass_isa.ReduceOp.max
                                              ).then_inc(amax_red, 1)
                    pool.wait_ge(amax_red, 2)
                s, c = divmod(n, NC)
                p0 = gh[s]
                pool.wait_ge(rmul_done, 2 * n + 2)
                m = rope_m[p0:p0 + DR, c % 2, :, :]
                pool.tensor_tensor(m[:, :, 0], m[:, :, 0], m[:, :, 1], ALU.add).then_inc(radd_done, 1)
            n = 0
            for g in range(NG):
                for c, kt, at, diagonal in columns(g):
                    if diagonal:
                        pool.wait_ge(exp_done, G4 * (n + 1))
                        p = probs[:, n % 3, :, at:at + PART]
                        pool.affine_select(out=p, in_=p, compare_op=ALU.is_ge, fill=0.0, base=0,
                                           pattern=[[0, G4], [1, PART]], channel_multiplier=-1
                                           ).then_inc(mask_done, 1)
                    n += 1

        @block.scalar
        def _(act):
            act.dma_start(pack[:, :], wpack).then_inc(ld_pack, 16)
            act.dma_start(rope_c[0:64, :], rope).then_inc(ld_rope, 16)
            act.dma_start(rope_c[64:128, :], rope).then_inc(ld_rope, 16)
            act.dma_start(b3_sb[:, :], b3).then_inc(ld_b3, 16)
            act.wait_ge(var_ready, 1)
            act.activation(ln[:, 1, :], ln[:, 0, :], ACT.Sqrt).then_inc(sqrt_done, 1)
            for c in range(NC):
                cols = slice(c * BANK, (c + 1) * BANK)
                act.wait_ge(xt_ready, c + 1)
                act.activation(x_hi[:, cols], bank(c), ACT.Copy).then_inc(xhi_done, 1)
                act.activation(x_t[:, cols], bank(c), ACT.Copy).then_inc(xt_done, 1)
            act.wait_ge(scales_ready, 1)
            for c in range(NC):
                act.wait_ge(q_ready, c + 1)
                act.activation(planes[:, QHI, c * BANK:(c + 1) * BANK], bank(4 + c), ACT.Copy, scale=ALPHA
                               ).then_inc(qhi_done, 1)
            for c in range(NC):
                act.wait_ge(c_ready, c + 1)
                act.activation(c_t[:, c * BANK:(c + 1) * BANK], bank(c), ACT.Copy).then_inc(ct_done, 1)

            def rope_hi(s):
                for c in range(NC):
                    p0 = gh[s]
                    act.wait_ge(radd_done, s * NC + c + 1)
                    act.activation(rope_s[p0:p0 + DR, c * BANK:(c + 1) * BANK], rope_m[p0:p0 + DR, c % 2, :, 0],
                                   ACT.Copy, scale=scales[p0:p0 + DR, s:s + 1]).then_inc(rhi_done, 1)

            rope_hi(0)
            for c in range(NC):
                act.wait_ge(k_ready, c + 1)
                act.activation(planes[:, KHI, c * BANK:(c + 1) * BANK], bank(c), ACT.Copy, scale=BETA
                               ).then_inc(khi_done, 1)
            rope_hi(1)
            act.wait_ge(ld_w12, 32)
            act.wait_ge(scales_ready, 2)
            for i, a in enumerate((A1, A2)):
                act.activation(w_hi[:, i, :], raw12[:, i, :], ACT.Copy, scale=a).then_inc(whi_done, 1)
            act.wait_ge(pool_const, 5)
            for c in range(NC):
                act.wait_ge(v_ready, c + 1)
                act.activation(v_aug[:, c * TPC:(c + 1) * TPC, :, 0:HD],
                               bank(c).rearrange("p (t h d) -> p t h d", t=TPC, h=NH), ACT.Copy).then_inc(v_done, 1)
            act.wait_ge(gap_ready, 1)
            act.activation(rw[:, 1, :], rw[:, 0, :], ACT.Exp).then_inc(gexp_done, 1)
            act.wait_ge(combt_ready, 1)
            for c in range(NC):
                act.activation(comb_t[:, c * BANK:(c + 1) * BANK], bank(c, p1=E), ACT.Copy).then_inc(combt_done, 1)
            act.wait_ge(scales_ready, 2)
            with act.Fori(0, E) as e:
                act.activation(b1_e[:, :], w("b1")[:, bass.ds(FJ * e, FJ)], ACT.Copy).then_inc(b1_done, 1)
                for u in range(NC * FJ):
                    j = u % FJ
                    if u == 0:
                        act.wait_ge(b1_done, e + 1)
                    act.wait_ge(up_g, NC * FJ * e + u + 1)
                    act.activation(silu[:, j, :], bank(j), ACT.Silu, bias=b1_e[:, j:j + 1],
                                   scale=IA1).then_inc(silu_done, 1)
                act.wait_ge(silu_done, NC * FJ * (e + 1))

            def output_rows(q):
                act.wait_ge(pv_done, NCOL * (q // CPB) + (TPC, NCOL)[q % CPB])
                if q >= 2:
                    act.wait_ge(ring_ready, ring_at["oT", (q - 2) // CPB, q % CPB] + 1)
                act.activation(o_sb[:, q % 2, :], bank(6 + q % 2), ACT.Copy).then_inc(o_done, 1)

            act.wait_ge(mix_done, 2 + E * NC)
            u = 0
            for g in range(NG):
                for k, (c, kt, at, _) in enumerate(columns(g)):
                    n = g * NCOL + k
                    for j in range(G4):
                        act.wait_ge(s_ready, u + 1)
                        if n >= 3 and j == 0:
                            act.wait_ge(pv_done, n - 2)
                        act.activation(probs[:, n % 3, j, at:BANK], bank(4 + u % 2, at), ACT.Exp, scale=GAMMA
                                       ).then_inc(exp_done, 1)
                        u += 1
                    if k == TPC:
                        output_rows(CPB * g)
                    if k == 0 and g:
                        output_rows(CPB * g - 1)
            output_rows(CPB * NG - 1)

        @block.tensor
        def _(pe):
            pe.wait_ge(pool_const, 3)
            for t in range(NT):
                pe.wait_ge(xn_ready, t + 1)
                mm = pe.transpose(bank(t // TPC, t % TPC * PART, t % TPC * PART + PART), xn[:, t, :], identf[:, :])
                if t % TPC == TPC - 1:
                    mm.then_inc(xt_ready, 1)
            pe.wait_ge(ld_pack, 16)
            for c in range(NC):
                pe.wait_ge(xt_done, c + 1)
                pe.matmul(bank(4 + c), w("wq"), x_t[:, c * BANK:(c + 1) * BANK], start=True, stop=True
                          ).then_inc(q_ready, 1)
            for c in range(NC):
                pe.wait_ge(xhi_done, c + 1)
                pe.wait_ge(xlo_done, c + 1)
                pe.matmul(bank(c), w("wkv"), x_t[:, c * BANK:(c + 1) * BANK], start=True, stop=True
                          ).then_inc(c_ready, 1)
            for c in range(NC):
                pe.wait_ge(qhi_done, c + 1)
                pe.wait_ge(qlo_done, c + 1)
                pe.matmul(bank(4 + c, p1=2 * DR), w("wqr"), x_t[:, c * BANK:(c + 1) * BANK], start=True, stop=True
                          ).then_inc(r_ready, 1)
            for c in range(NC):
                pe.wait_ge(ct_done, c + 1)
                pe.matmul(bank(c), w("wk"), c_t[:, c * BANK:(c + 1) * BANK], start=True, stop=True
                          ).then_inc(k_ready, 1)
            for c in range(NC):
                pe.wait_ge(rmul_done, 2 * c + 2)
                pe.matmul(bank(4 + c, p0=64, p1=64 + 2 * DR), w("wkr"), c_t[:, c * BANK:(c + 1) * BANK],
                          start=True, stop=True).then_inc(r_ready, 1)
            for c in range(NC):
                pe.wait_ge(khi_done, c + 1)
                pe.wait_ge(klo_done, c + 1)
                for t in range(TPC):
                    at = (c * TPC + t) * PART
                    mm = pe.matmul(bank(c, t * PART, (t + 1) * PART), c_t[:, at:at + PART], w("wv"),
                                   start=True, stop=True)
                mm.then_inc(v_ready, 1)
            pe.wait_ge(rmul_done, 2 * NC + 2)
            for t in range(NT):
                mm = pe.matmul(bank(4, t * E, (t + 1) * E), x_t[:, t * PART:(t + 1) * PART], w("wg"),
                               start=True, stop=True)
            mm.then_inc(gate_ready, 1)
            pe.wait_ge(v_done, NC)
            pe.wait_ge(comb_ready, 1)
            for t in range(NT):
                mm = pe.transpose(bank(t // TPC, t % TPC * PART, t % TPC * PART + PART, p1=E), comb[:, t, :],
                                  identf[:, :])
            mm.then_inc(combt_ready, 1)
            pe.wait_ge(combt_done, NC)
            pe.wait_ge(rmul_done, 4 * NC)

            def up(e, c):
                cols = slice(c * BANK, (c + 1) * BANK)
                for j in range(FJ):
                    pe.wait_ge(hid_done, NC * FJ * e + FJ * c + j + 1)
                    pe.wait_ge(wlo_done, 2)
                    for i, ready in enumerate((up_g, up_v)):
                        dst = bank(2 * i + j)
                        hi = w_hi[:, i, bass.ds(e * FF + j * PART, PART)]
                        lo = w_lo[:, i, bass.ds(e * FF + j * PART, PART)]
                        pe.matmul(dst, hi, x_hi[:, cols], start=True, stop=False)
                        pe.matmul(dst, hi, x_lo[:, cols], start=False, stop=False)
                        pe.matmul(dst, lo, x_hi[:, cols], start=False, stop=True).then_inc(ready, 1)

            def down(e, c):
                pe.wait_ge(hid_done, 2 + NC * FJ * e + FJ * c + 2)
                pe.wait_ge(mix_done, NC * e + c + 1)
                for t in range(TPC):
                    for j in range(FJ):
                        mm = pe.matmul(bank(4 + c % 2, t * PART, (t + 1) * PART),
                                       hid[:, c % 2, j, t * PART:(t + 1) * PART],
                                       w3_sb[:, bass.ds((FJ * e + j) * D, D)], start=(j == 0), stop=(j == FJ - 1))
                mm.then_inc(down_ready, 1)

            pe.sem_inc(down_ready, 2)
            pe.wait_ge(whi_done, 2)
            pe.wait_ge(wlo_done, 2)
            pe.wait_ge(ld_w3, 16)
            up(0, 0)
            with pe.Fori(0, E - 1) as e:
                for c in range(NC):
                    up(*((e, c + 1) if c + 1 < NC else (e + 1, 0)))
                    down(e, c)
            for c in range(NC):
                if c + 1 < NC:
                    up(E - 1, c + 1)
                down(E - 1, c)

            def ring_job(item):
                r = ring_at[item]
                kind = item[0]
                b0 = 2 * (r % 2)
                if r >= 2:
                    pe.wait_ge(ring_done, r - 1)
                if kind == "max1":
                    _, g, j, i = item
                    slot = G4 * (g % GPB) + j
                    q = stack(slot, (0, QK_ROWS), 0, i * PART, (i + 1) * PART)
                    end = (i + 1) * PART
                    pe.matmul(bank(b0), q, stack(slot, (0, QK_ROWS), 1, 0, BANK), start=True, stop=True)
                    pe.matmul(bank(b0 + 1, 0, end - BANK), q, stack(slot, (0, QK_ROWS), 1, BANK, end),
                              start=True, stop=False)
                    mm = pe.matmul(bank(b0 + 1, end - BANK - PART, end - BANK), identb[:, :], causal[:, :],
                                   start=False, stop=True)
                elif kind == "max2":
                    _, g, j, i = item
                    end = (i + 1) * PART
                    for k in range(2):
                        slot = G4 * (g % GPB) + j + k
                        pe.matmul(bank(b0 + k, 0, end), stack(slot, (0, QK_ROWS), 0, i * PART, end),
                                  stack(slot, (0, QK_ROWS), 1, 0, end), start=True, stop=False)
                        mm = pe.matmul(bank(b0 + k, end - PART, end), identb[:, :], causal[:, :],
                                       start=False, stop=True)
                elif kind == "mT":
                    g = item[1]
                    pe.wait_ge(msplit_done, 2 * g + 2)
                    n = 2 * G4 * KT
                    mm = pe.transpose(bank(b0, 0, PART // 2, p1=n).bitcast(F16),
                                      max_s[:, g % 2].rearrange("p s j i -> p (s j i)"), identh[:, :])
                elif kind == "oT":
                    q = item[1] * CPB + item[2]
                    pe.wait_ge(o_done, q + 1)
                    for t in range(TPC):
                        mm = pe.transpose(bank(b0, t * PART, (t + 1) * PART),
                                          o_sb[:, q % 2, t * PART:(t + 1) * PART], identf[:, :])
                elif kind == "aT":
                    _, b, c = item
                    pe.wait_ge(ring_done, ring_at["oT", GPB * (b + 1) - 1, c] + 1)
                    for t in range(TPC):
                        mm = pe.transpose(bank(b0, t * PART, (t + 1) * PART), attn[:, b, c * TPC + t, :],
                                          identf[:, :])
                else:
                    _, b, c = item
                    pe.wait_ge(ring_done, ring_at["aT", b, c] + 1)
                    for t in range(TPC):
                        tile = b * KT + c * TPC + t
                        pe.matmul(bank(b0, t * PART, (t + 1) * PART), attn_t[:, c, t * PART:(t + 1) * PART],
                                  w("wo"), start=True, stop=False)
                        mm = pe.matmul(bank(b0, t * PART, (t + 1) * PART),
                                       comb_t[:, tile * PART:(tile + 1) * PART], b3_sb[:, :],
                                       start=False, stop=True)
                mm.then_inc(ring_ready, 1)

            def prob_values(n):
                g, k = divmod(n, NCOL)
                c, kt, at, diagonal = columns(g)[k]
                pe.wait_ge(exp_done, G4 * (n + 1))
                if diagonal:
                    pe.wait_ge(mask_done, masks[n])
                q = CPB * g + c
                if kt == 0 and q >= 2:
                    pe.wait_ge(o_done, q - 1)
                tile = KT * (g // GPB) + kt
                for j in range(G4):
                    mm = pe.matmul(bank(6 + q % 2, at, BANK, p0=32 * j, p1=32 * j + 32),
                                   v_aug[:, tile, G4 * (g % GPB) + j, :], probs[:, n % 3, j, at:BANK],
                                   start=(kt == 0), stop=(kt == TPC * (c + 1) - 1))
                mm.then_inc(pv_done, 1)

            masks, found = {}, 0
            for n in range(NG * NCOL):
                if columns(0)[n % NCOL][3]:
                    found += 1
                    masks[n] = found

            pe.wait_ge(hid_done, 2 + E * NC * FJ)
            pe.wait_ge(mix_done, 2 + E * NC)
            pe.wait_ge(ld_b3, 16)
            loads = {}

            def stacks_loaded(g):
                if g not in loads:
                    loads[g] = True
                    pe.wait_ge(load[g], 16 * (4 + (g < GPB) + 4 * G4))

            def run_ring(items):
                for item in items:
                    if item[0] in ("max1", "max2"):
                        stacks_loaded(item[1])
                    ring_job(item)

            run_ring(first)
            u = 0
            for g in range(NG):
                pe.wait_ge(mrow[g], 16 * 2 * G4)
                for k, (c, kt, at, _) in enumerate(columns(g)):
                    n = g * NCOL + k
                    ring = slots[n]
                    half = (len(ring) + 1) // 2
                    for j in range(G4):
                        slot = G4 * (g % GPB) + j
                        if u >= 2:
                            pe.wait_ge(exp_done, u - 1)
                        pe.matmul(bank(4 + u % 2, at), stack(slot, (0, ALL_ROWS), 1, kt * PART, (kt + 1) * PART),
                                  stack(slot, (0, ALL_ROWS), 0, c * BANK + at, (c + 1) * BANK),
                                  start=True, stop=True).then_inc(s_ready, 1)
                        u += 1
                        if j == 1:
                            run_ring(ring[:half])
                        if j == 2 and n:
                            prob_values(n - 1)
                    run_ring(ring[half:])
            prob_values(NG * NCOL - 1)
            run_ring(tail)

        @block.vector
        def _(dve):
            chained = [0]

            def step(ins):
                chained[0] += 1
                return ins.then_inc(dve_chain, 1)

            def settle():
                dve.wait_ge(dve_chain, chained[0])

            for c in range(NC):
                dve.wait_ge(ld_x[c], 16)
                for t in range(c * TPC, (c + 1) * TPC):
                    step(dve.bn_stats(stats[:, t, :], acc[:, t, :]))
                if c == 0:
                    dve.wait_ge(ld_pack, 16)
                    for n, (a, b) in enumerate((("wq", "wqr"), ("wkv", "wkv"), ("wk", "wkr"))):
                        dve.tensor_reduce(amax[:, n:n + 1], pack[:, PACK[a][0]:PACK[b][1]], AX.X, ALU.max,
                                          apply_absolute_value=True).then_inc(amax_done, 1)
            settle()
            for t in range(NT):
                step(dve.bn_aggr(mv[:, t, :], stats[:, t, :]))
            settle()
            dve.tensor_scalar(ln[:, 0, :], mv[:, :, 1], EPS, None, ALU.add).then_inc(var_ready, 1)
            def powers(a, b):
                step(dve.tensor_scalar(pow2[:, a:b], amax_all[:, a:b], 2.0 ** -30, None, ALU.max))
                settle()
                step(dve.tensor_scalar(pow2[:, a:b].bitcast(I32), pow2[:, a:b].bitcast(I32), 0x7F800000, None,
                                       ALU.bitwise_and))
                settle()
                step(dve.reciprocal(ipow[:, a:b], pow2[:, a:b]))
                settle()
            dve.wait_ge(amax_red, 1)
            powers(0, 3)
            step(dve.tensor_scalar(ALPHA, ipow[:, 0:1], 2.0 ** 4, None, ALU.mult))
            step(dve.tensor_scalar(BETA, ipow[:, 1:2], ipow[:, 2:3], 2.0 ** -4, ALU.mult, ALU.mult))
            step(dve.tensor_scalar(TMP, pow2[:, 0:1], pow2[:, 1:2], None, ALU.mult))
            settle()
            step(dve.tensor_scalar(GAMMA, TMP, pow2[:, 2:3], float(np.float32(1.0) / np.sqrt(np.float32(HD + DR))),
                                   ALU.mult, ALU.mult))
            settle()
            dve.sem_inc(scales_ready, 1)
            dve.wait_ge(sqrt_done, 1)
            step(dve.reciprocal(ln[:, 2, :], ln[:, 1, :]))
            settle()
            step(dve.tensor_tensor(ln[:, 3, :], ln[:, 0, :], ln[:, 2, :], ALU.mult))
            settle()
            step(dve.tensor_tensor(ln[:, 4, :], ln[:, 3, :], ln[:, 1, :], ALU.add))
            settle()
            step(dve.tensor_scalar(ln[:, 2, :], ln[:, 4, :], 0.5, None, ALU.mult))
            settle()
            step(dve.reciprocal(ln[:, 5, :], ln[:, 2, :]))
            settle()
            for t in range(NT):
                dve.tensor_scalar(xn[:, t, :], acc[:, t, :], mv[:, t, 0:1], ln[:, 5, t:t + 1], ALU.subtract, ALU.mult
                                  ).then_inc(xn_ready, 1)
            for c in range(NC):
                cols = slice(c * BANK, (c + 1) * BANK)
                dve.wait_ge(xt_done, c + 1)
                dve.tensor_tensor(x_lo[:, cols], bank(c), x_hi[:, cols], ALU.subtract).then_inc(xlo_done, 1)
            def low(plane_lo, plane_hi, b0, scale, hi_done, done):
                for c in range(NC):
                    cols = slice(c * BANK, (c + 1) * BANK)
                    dve.wait_ge(hi_done, c + 1)
                    dve.scalar_tensor_tensor(out=planes[:, plane_lo, cols], in0=bank(b0 + c), scalar=scale,
                                             in1=planes[:, plane_hi, cols], op0=ALU.mult, op1=ALU.subtract
                                             ).then_inc(done, 1)

            def rope_low(s, c):
                p0 = gh[s]
                cols = slice(c * BANK, (c + 1) * BANK)
                dve.wait_ge(rhi_done, s * NC + c + 1)
                dve.scalar_tensor_tensor(out=rope_s[p0 + DR:p0 + 2 * DR, cols], in0=rope_m[p0:p0 + DR, c % 2, :, 0],
                                         scalar=scales[p0:p0 + DR, s:s + 1], in1=rope_s[p0:p0 + DR, cols],
                                         op0=ALU.mult, op1=ALU.subtract).then_inc(rlo_done, 1)

            def rotate(s):
                p0 = gh[s]
                for c in range(NC):
                    dve.wait_ge(r_ready, s * NC + c + 1)
                    if c >= 2:
                        rope_low(s, c - 2)
                        dve.wait_ge(rlo_done, s * NC + c - 1)
                    at = c % CPB * BANK
                    for m in range(2):
                        q0 = p0 + m * DR
                        dve.tensor_tensor(rope_m[p0:p0 + DR, c % 2, :, m], bank(4 + c, p0=q0, p1=q0 + DR),
                                          rope_c[q0:q0 + DR, at:at + BANK], ALU.mult).then_inc(rmul_done, 1)
                rope_low(s, NC - 2)
                rope_low(s, NC - 1)

            low(QLO, QHI, 4, ALPHA, qhi_done, qlo_done)
            dve.wait_ge(ld_rope, 32)
            rotate(0)
            low(KLO, KHI, 0, BETA, khi_done, klo_done)
            dve.wait_ge(ld_w12, 32)
            for i in range(2):
                dve.tensor_reduce(amax[:, 3 + i:4 + i], raw12[:, i, :], AX.X, ALU.max,
                                  apply_absolute_value=True).then_inc(amax_done, 1)
            rotate(1)
            dve.wait_ge(amax_red, 2)
            powers(3, 5)
            for n, (a, ia) in enumerate(((A1, IA1), (A2, IA2))):
                step(dve.tensor_scalar(a, ipow[:, 3 + n:4 + n], 2.0 ** 13, None, ALU.mult))
                step(dve.tensor_scalar(ia, pow2[:, 3 + n:4 + n], 2.0 ** -13, None, ALU.mult))
            settle()
            dve.sem_inc(scales_ready, 1)
            step(dve.tensor_scalar(b2_s[:, :], w("b2"), A2, None, ALU.mult))
            dve.wait_ge(gate_ready, 1)
            step(dve.tensor_copy(logit[:, :, :], bank(4, 0, NT * E).rearrange("p (t e) -> p t e", e=E)))
            settle()
            for t in range(NT):
                step(dve.max(top[:, t, :], logit[:, t, :]))
            settle()
            dve.tensor_tensor(rw[:, 0, :], top[:, :, 1], top[:, :, 0], ALU.subtract).then_inc(gap_ready, 1)
            for t in range(NT):
                step(dve.max_index(topi[:, t, :], top[:, t, :], logit[:, t, :]))
            settle()
            step(dve.tensor_copy(topf[:, :, :], topi[:, :, :]))
            dve.wait_ge(gexp_done, 1)
            step(dve.tensor_scalar(rw[:, 2, :], rw[:, 1, :], 1.0, None, ALU.add))
            settle()
            step(dve.reciprocal(rw[:, 3, :], rw[:, 2, :]))
            settle()
            step(dve.tensor_tensor(rw[:, 2, :], rw[:, 1, :], rw[:, 3, :], ALU.mult))
            for n in range(2):
                step(dve.tensor_tensor(eq[:, n], topf[:, :, n:n + 1].broadcast_to([PART, NT, E]),
                                       w("iota").unsqueeze(1).broadcast_to([PART, NT, E]), ALU.is_equal))
            settle()
            for n in range(2):
                step(dve.tensor_tensor(eq[:, n], eq[:, n],
                                       rw[:, 3 - n, :].unsqueeze(2).broadcast_to([PART, NT, E]), ALU.mult))
            settle()
            dve.tensor_tensor(comb[:, :, :], eq[:, 0], eq[:, 1], ALU.add).then_inc(comb_ready, 1)
            dve.wait_ge(comb_ready, 1)
            step(dve.tensor_scalar(comb_s[:, :, :], comb[:, :, :], IA2, None, ALU.mult))
            for i, a in enumerate((A1, A2)):
                dve.wait_ge(whi_done, i + 1)
                dve.scalar_tensor_tensor(out=w_lo[:, i, :], in0=raw12[:, i, :], scalar=a, in1=w_hi[:, i, :],
                                         op0=ALU.mult, op1=ALU.subtract).then_inc(wlo_done, 1)
            settle()

            def hidden(e, c):
                for j in range(FJ):
                    n = NC * FJ * e + FJ * c + j
                    dve.wait_ge(silu_done, n + 1)
                    dve.wait_ge(up_v, n + 1)
                    dve.wait_ge(down_ready, NC * e + c + 1)
                    dve.scalar_tensor_tensor(out=hid[:, c % 2, j, :], in0=bank(2 + j),
                                             scalar=b2_s[:, bass.ds(FJ * e + j, 1)], in1=silu[:, j, :],
                                             op0=ALU.add, op1=ALU.mult).then_inc(hid_done, 1)

            def mix(e, c):
                dve.wait_ge(down_ready, 2 + NC * e + c + 1)
                dve.wait_ge(mix_done, NC * e + c + 1)
                for t in range(TPC):
                    tile = c * TPC + t
                    mm = dve.scalar_tensor_tensor(out=acc[:, tile, :], in0=bank(4 + c % 2, t * PART, (t + 1) * PART),
                                                  scalar=comb_s[:, tile, bass.ds(e, 1)], in1=acc[:, tile, :],
                                                  op0=ALU.mult, op1=ALU.add)
                mm.then_inc(mix_done, 1)

            dve.sem_inc(hid_done, 2)
            dve.sem_inc(mix_done, 2)
            hidden(0, 0)
            with dve.Fori(0, E - 1) as e:
                for c in range(NC):
                    hidden(*((e, c + 1) if c + 1 < NC else (e + 1, 0)))
                    mix(e, c)
            for c in range(NC):
                if c + 1 < NC:
                    hidden(E - 1, c + 1)
                mix(E - 1, c)

            def ring_result(item):
                r = ring_at[item]
                kind = item[0]
                b0 = 2 * (r % 2)
                dve.wait_ge(ring_ready, r + 1)
                if kind == "max1":
                    _, g, j, i = item
                    if g >= 2 and (j, i) == (0, KT - 1):
                        dve.wait_ge(msplit_done, 2 * (g - 1))
                    ins = dve.tensor_reduce(maxima[:, g % 2, j, i:i + 1],
                                            ps[:, b0 * BANK:b0 * BANK + (i + 1) * PART], AX.X, ALU.max)
                elif kind == "max2":
                    _, g, j, i = item
                    pair = ps[:, b0 * BANK:(b0 + 2) * BANK].rearrange("p (k n) -> p k n", k=2)
                    ins = dve.tensor_reduce(maxima[:, g % 2, j:j + 2, i], pair[:, :, 0:(i + 1) * PART], AX.X, ALU.max)
                elif kind == "mT":
                    g = item[1]
                    if g >= 2:
                        dve.wait_ge(mrow[g - 2], 16 * 2 * G4)
                    ins = dve.tensor_copy(max_t[:, g % 2, :], bank(b0, 0, PART // 2, p1=2 * G4 * KT).bitcast(F16))
                elif kind == "oT":
                    _, g, c = item
                    q = g * CPB + c
                    o = bank(b0).rearrange("p (t j d) -> p t j d", t=TPC, j=G4)
                    step(dve.reciprocal(rden[:, q % 2], o[:, :, :, HD]))
                    settle()
                    h0 = G4 * HD * (g % GPB)
                    dst = attn[:, g // GPB, c * TPC:(c + 1) * TPC, h0:h0 + G4 * HD]
                    ins = dve.tensor_tensor(dst.rearrange("p t (j d) -> p t j d", j=G4), o[:, :, :, 0:HD],
                                            rden[:, q % 2].unsqueeze(3).broadcast_to([PART, TPC, G4, HD]), ALU.mult)
                elif kind == "aT":
                    _, b, c = item
                    ins = dve.tensor_copy(attn_t[:, c, :], bank(b0))
                else:
                    _, b, c = item
                    tiles = slice(b * KT + c * TPC, b * KT + (c + 1) * TPC)
                    ins = dve.tensor_tensor(acc[:, tiles, :], acc[:, tiles, :],
                                            bank(b0).rearrange("p (t d) -> p t d", t=TPC), ALU.add)
                ins.then_inc(ring_done, 1)
                if kind == "max2" and item[2:] == (G4 - 2, TPC - 1):
                    g = item[1]
                    dve.wait_ge(ring_done, r + 1)
                    m = maxima[:, g % 2]
                    if g >= 2:
                        dve.wait_ge(ring_ready, ring_at["mT", g - 2] + 1)
                    dve.tensor_scalar(max_s[:, g % 2, 0], m, -1.0 / KAPPA, None, ALU.mult).then_inc(msplit_done, 1)
                    dve.wait_ge(msplit_done, 2 * g + 1)
                    dve.scalar_tensor_tensor(out=max_s[:, g % 2, 1], in0=m, scalar=-1.0 / KAPPA,
                                             in1=max_s[:, g % 2, 0], op0=ALU.mult, op1=ALU.subtract
                                             ).then_inc(msplit_done, 1)

            dve.wait_ge(mix_done, 2 + E * NC)
            for item in ring_order:
                ring_result(item)


def kernel(**inputs):
    import concourse.bacc as bacc
    from concourse.bass_utils import run_bass_kernel_spmd

    a = {k: np.asarray(v) for k, v in inputs.items()}
    h = DR // 2

    def both(wr):
        return np.concatenate([wr, wr[:, h:], wr[:, :h]], axis=1)

    def by_half(b):
        return b.reshape(E, FJ, PART).transpose(2, 0, 1).reshape(PART, E * FJ)

    f32 = np.float32
    freq = (f32(1.0) / np.power(f32(10000.0), np.arange(0, DR, 2, dtype=f32) / f32(DR))).astype(f32)
    angle = np.outer(np.arange(T, dtype=f32), freq).astype(f32)
    cos, sin = np.cos(angle).T, np.sin(angle).T
    pack = np.concatenate([
        a["L0_attn_W_q"], both(a["L0_attn_W_q_rope"]), a["L0_attn_W_kv_down"], a["L0_attn_W_k_up"],
        both(a["L0_attn_W_k_rope"]), a["L0_attn_W_v_up"], a["L0_attn_W_o"], a["L0_ffn_Wg"].T,
        by_half(a["L0_ffn_b1"]), by_half(a["L0_ffn_b2"]),
        np.broadcast_to(np.arange(E, dtype=f32), (PART, E))], axis=1)
    arrays = {
        "x": a["L0_attn_x"].reshape(TOK, D),
        "wpack": pack,
        "w12": np.stack([a["L0_ffn_W1"].transpose(2, 0, 1).reshape(D, E * FF),
                         a["L0_ffn_W2"].transpose(2, 0, 1).reshape(D, E * FF)]),
        "w3": a["L0_ffn_W3"].reshape(E, D, FJ, PART).transpose(3, 0, 2, 1).reshape(PART, E * FJ * D),
        "b3": a["L0_ffn_b3"],
        "rope": np.concatenate([cos, cos, -sin, sin], axis=0),
    }
    arrays = {k: np.ascontiguousarray(v) for k, v in arrays.items()}
    nc = bacc.Bacc("TRN2", target_bir_lowering=False, num_devices=1)
    args = [nc.dram_tensor(k, v.shape, mybir.dt.from_np(v.dtype), kind="ExternalInput").ap()
            for k, v in arrays.items()]
    out = nc.dram_tensor("out", (TOK, D), F32, kind="ExternalOutput").ap()
    build(nc, *args, out)
    r = run_bass_kernel_spmd(nc, [arrays], core_ids=[0])
    return r.results[0]["out"].reshape(B, T, D)
```

```python
from contextlib import ExitStack

import numpy as np
import concourse.bass as bass
from concourse import mybir

F32 = mybir.dt.float32
F16 = mybir.dt.float16
BF16 = mybir.dt.bfloat16
I32 = mybir.dt.int32
U32 = mybir.dt.uint32
ALU = mybir.AluOpType
ACT = mybir.ActivationFunctionType
AX = mybir.AxisListType

PART = 128
BANK = 512
B, T, D = 2, 1024, 128
NH, HD, DR = 16, 8, 32
E, FF = 8, 256
TOK = B * T
NT = TOK // PART
NC = TOK // BANK
TPC = BANK // PART
FJ = FF // PART
G4 = 4
GPB = NH // G4
NG = B * GPB
KT = T // PART
CPB = T // BANK
EPS = 1e-5
KAPPA = 2.0 ** 15
QK_SCALE = 2.0 ** 8
EXP_SCALE = np.float32(1.0) / np.sqrt(np.float32(HD + DR)) / np.float32(QK_SCALE)
NEG = -1e30
HROW, RROW = 3 * HD, 3 * DR
QK_ROWS = HROW + RROW
ALL_ROWS = QK_ROWS + 2

PACK = {}
_at = 0
for _name, _n in (("wq", D), ("wqr", 2 * DR), ("wkv", D), ("wk", D), ("wkr", 2 * DR), ("wv", D), ("wo", D),
                  ("wg", E), ("b1", E * FJ), ("b2", E * FJ), ("iota", 32)):
    PACK[_name] = (_at, _at + _n)
    _at += _n
PACK_COLS = _at

QLO, KHI, QHI, KLO = range(4)

TOPK = 2
SLOT = 2 * PART
SH = SLOT // PART
SLOTS = 2 * -(-(TOK * TOPK // SLOT + E - 1) // 2)
TAB = SLOTS + 2
assert TAB <= 32 and TOK == E * SLOT
XIN = 4
YIN = 16


def columns(g):
    out = []
    for c in range(CPB):
        for kt in range(TPC * (c + 1)):
            out.append((c, kt, max(0, kt * PART - c * BANK), kt >= c * TPC))
    return out


NCOL = len(columns(0))


MID = GPB * NCOL
SCATTER0 = 8
XT0 = 34


def spread(start):
    out, m, n = {}, 0, start
    while m < TOPK * NT:
        k = 2 if start < MID or not columns(0)[n % NCOL][3] else 1
        out[n] = list(range(m, min(m + k, TOPK * NT)))
        m += k
        n += 1
    return out


SCATTERS, GATHERS = spread(SCATTER0), spread(MID)
SCATTERED = max(SCATTERS) + 1


def max_items(g, c):
    if c:
        return [("max1", g, j, i) for j in range(G4) for i in range(KT - 1, TPC - 1, -1)]
    return [("max2", g, j, i) for j in range(0, G4, 2) for i in range(TPC)]


NMAX = sum(len(max_items(0, c)) for c in range(CPB))


def schedule():
    stream, last = [], None
    for g in range(NG):
        for c in range(CPB):
            items = max_items(g, c)
            if last:
                items.insert(2, ("mT", *last))
            stream += items
            last = g, c
    stream.append(("mT", *last))
    ahead = stream.index(("mT", 0, 0)) + 1 + 5
    first, rest = stream[:ahead], stream[ahead:]
    slots = []
    given = turned = 0
    taken = sum(item[0] != "mT" for item in first)
    for n in range(NG * NCOL):
        want = (16, 20, 24)[n] if n < 3 else NMAX + 3 + 2.1 * (n - 2)
        here = []
        while given < len(rest) and (taken < want or rest[given][0] == "mT"):
            here.append(rest[given])
            taken += rest[given][0] != "mT"
            given += 1
        g, k = divmod(n, NCOL)
        if n == 2:
            here.append(("count",))
        if XT0 <= n < MID:
            want = SLOTS * (n + 1 - XT0) // (MID - XT0)
            here += [("turn", s) for s in range(turned, want)]
            turned = want
        if n == NG * NCOL - NCOL:
            here += [("cT", B - 1, 0)]
        if NG * NCOL - 5 <= n < NG * NCOL - 2:
            here += [[("aT", B - 1, 0)], [("wo", B - 1, 0)], [("cT", B - 1, 1)]][n - (NG * NCOL - 5)]
        if g % GPB == 0 and g and 2 <= k < 6:
            b, c = g // GPB - 1, (k - 2) // 2
            here += [("aT", b, c), ("cT", b, c)] if k % 2 == 0 else [("wo", b, c)]
        if k == TPC + 1:
            here.append(("oT", g, 0))
        if k == 1 and g:
            here.append(("oT", g - 1, 1))
        slots.append(here)
    tail = [("oT", NG - 1, 1)] + [("aT", B - 1, 1), ("wo", B - 1, 1)]
    return first, slots, tail


def score_banks(slots):
    last = max(n for n in range(NG * NCOL) if any(item[0] in ("max1", "max2", "mT") for item in slots[n]))
    banks = []
    for n in range(NG * NCOL):
        for j in range(G4):
            banks.append((4, 5, 0, 1)[j] if n > last else 4 + j % 2)
    return last, banks


def build(nc, x, wpack, w12, w3, b3, rope, kappa, out):
    first, slots, tail = schedule()
    ring_order = first + [i for s in slots for i in s] + tail
    ring_at = {item: r for r, item in enumerate(ring_order)}
    last_max, sbank = score_banks(slots)
    wide_ring = len(first) + sum(len(s) for s in slots[:last_max + 1])

    def ring_bank(r):
        return 2 * (r % 2) if r < wide_ring else 2

    mid_ring = len(first) + sum(len(s) for s in slots[:MID])
    qkbuf = nc.dram_tensor("qkbuf", [B, NH, HD, 4 * T], F16).ap()
    maxbuf = nc.dram_tensor("maxbuf", [NG, CPB, 2, G4, BANK], F16).ap()
    xbuf = nc.dram_tensor("xbuf", [SLOTS * SLOT, 2 * D], F16).ap()
    ybuf = nc.dram_tensor("ybuf", [SLOTS * SLOT, D], F32).ap()

    with ExitStack() as ctx:
        def sb(name, shape, dt, scope=ctx):
            return scope.enter_context(nc.sbuf_tensor(name, shape, dt))

        def sem(name):
            return ctx.enter_context(nc.semaphore(name))

        acc = sb("acc", [PART, NT, D], F32)
        pack = sb("pack", [PART, PACK_COLS], F32)
        b3_sb = sb("b3_sb", [E, D], F32)
        identf = sb("identf", [PART, PART], F32)
        identh = sb("identh", [PART, PART], F16)
        identb = sb("identb", [PART, PART], BF16)
        causal = sb("causal", [PART, PART], BF16)
        before = sb("before", [PART, PART], F16)
        ones_h = sb("ones_h", [PART, PART], F16)
        zeros = sb("zeros", [PART, 2 * D], F16)
        v_aug = sb("v_aug", [PART, NT, NH, HD + 1], F32)
        rope_s = sb("rope_s", [PART, TOK], F16)
        stack_a = sb("stack_a", [PART, G4, 2, T], F16)
        w_hi = sb("w_hi", [D, 2, E * FF], F16)
        w_lo = sb("w_lo", [D, 2, E * FF], F16)
        w3_sb = sb("w3_sb", [PART, E * FJ * D], F32)
        xin = sb("xin", [PART, XIN, SH, 2 * D], F16)
        comb = sb("comb", [PART, NT, E], F32)
        comb_t = sb("comb_t", [E, BANK], F32)
        wmix = sb("wmix", [PART, TOPK, NT], F32)
        rows_i = sb("rows_i", [PART, TOPK * NT], U32)
        etab = sb("etab", [PART, TAB], I32)
        b1_t = sb("b1_t", [PART, FJ, TAB], F32)
        b2_t = sb("b2_t", [PART, FJ, TAB], F32)
        b1_e = sb("b1_e", [PART, 2, FJ], F32)
        attn = sb("attn", [PART, KT, D], F32)
        attn_t = sb("attn_t", [D, CPB, BANK], F32)
        o_sb = sb("o_sb", [PART, 2, BANK], F32)
        rden = sb("rden", [PART, 2, TPC, G4], F32)
        maxima = sb("maxima", [PART, 2, G4, KT], F32)
        max_s = sb("max_s", [PART, 2, CPB, 2, G4, TPC], F16)
        max_t = sb("max_t", [2 * G4 * TPC, CPB, PART], F16)
        amax = sb("amax", [PART, 8], F32)
        amax_all = sb("amax_all", [PART, 8], F32)
        pow2 = sb("pow2", [PART, 8], F32)
        ipow = sb("ipow", [PART, 8], F32)
        scales = sb("scales", [PART, 10], F32)
        ALPHA, BETA, TMP, A1, IA1, A2, IA2, TMP2 = (scales[:, i:i + 1] for i in range(8))
        b2_s = sb("b2_s", [PART, E * FJ], F32)
        logit = sb("logit", [PART, NT, E], F32)
        top = sb("top", [PART, NT, 8], F32)
        topi = sb("topi", [PART, NT, 8], U32)
        topf = sb("topf", [PART, NT, 8], F32)
        rw = sb("rw", [PART, 4, NT], F32)
        eq = sb("eq", [PART, TOPK, NT, E], F32)
        sel = sb("sel", [PART, NT, E], F16)
        pos = sb("pos", [PART, NT, E], F32)
        picked = sb("picked", [PART, TOPK, NT, E], F32)
        rows_f = sb("rows_f", [PART, TOPK, NT], F32)
        slot_e = sb("slot_e", [PART, 2, TAB, E], F32)
        slot_f = sb("slot_f", [PART, 2, TAB], F32)
        small = sb("small", [PART, 2, E, E], F32)
        per_e = sb("per_e", [PART, 6, E], F32)

        planes1 = sb("planes1", [PART, 4, T], F16)
        with ExitStack() as scope:
            planes = [sb("planes0", [PART, 4, T], F16, scope), planes1]
        with ExitStack() as scope:
            hid = sb("hid", [PART, 2, FJ, SLOT], F32, scope)
            silu = sb("silu", [PART, 2, FJ, SLOT], F32, scope)
        y_in = sb("y_in", [PART, YIN, D], F32)
        with ExitStack() as scope:
            raw12 = sb("raw12", [D, 2, E * FF], F32, scope)
            x_rows = sb("x_rows", [PART, NT, 2 * D], F16, scope)
        xs = sb("xs", [PART, SLOTS, 2 * SLOT], F16)
        ys = xs[:, :, :].bitcast(F32)
        with ExitStack() as scope:
            c_t = sb("c_t", [D, TOK], F32, scope)
            rope_m = sb("rope_m", [PART, 2, NT, 2 * DR], F32, scope)
            rope_sum = sb("rope_sum", [PART, 2, NT, DR], F32, scope)
            rope_hl = sb("rope_hl", [PART, NT, 4, DR], F16, scope)
            rope_c = sb("rope_c", [PART, KT, 2 * DR], F32, scope)
            stats = sb("stats", [PART, NT, 6], F32, scope)
            mv = sb("mv", [PART, NT, 2], F32, scope)
            ln = sb("ln", [PART, 6, NT], F32, scope)
            used = 4 * (TOK + 2 * NT * 2 * DR + 2 * NT * DR + NT * 2 * DR + KT * 2 * DR + 14 * NT)
            sb("gap", [PART, (NH - G4) * 2 * T // 2 - used // 4], F32, scope)
            xn = sb("xn", [PART, NT, D], F32, scope)
            x_t = sb("x_t", [D, TOK], F32, scope)
        stack_b = sb("stack_b", [PART, NH - G4, 2, T], F16)
        probs = sb("probs", [PART, 3, G4, BANK], F32)

        ps = ctx.enter_context(nc.psum_tensor("ps", [PART, 8 * BANK], F32))

        def bank(n, a=0, b=BANK, p0=0, p1=PART):
            return ps[p0:p1, n * BANK + a:n * BANK + b]

        def plane(which, c):
            return planes[c // CPB][:, which, c % CPB * BANK:(c % CPB + 1) * BANK]

        def w(name):
            return pack[:, PACK[name][0]:PACK[name][1]]

        def stack(slot, rows, part, a=0, b=T):
            if slot < G4:
                return stack_a[rows[0]:rows[1], slot, part, a:b]
            return stack_b[rows[0]:rows[1], slot - G4, part, a:b]

        def stacks(first_slot, rows, part):
            if first_slot < G4:
                return stack_a[rows[0]:rows[1], :, part, :]
            return stack_b[rows[0]:rows[1], first_slot - G4:first_slot, part, :]

        ld_x = [sem(f"ld_x{c}") for c in range(NC)]
        ld_pack, ld_w12, ld_w3, ld_b3, ld_rope = (sem(n) for n in ("ld_pack", "ld_w12", "ld_w3", "ld_b3", "ld_rope"))
        pool_const = sem("pool_const")
        amax_done = sem("amax_done")
        amax_red = sem("amax_red")
        dve_chain = sem("dve_chain")
        pool_chain = sem("pool_chain")
        scales_ready = sem("scales_ready")
        var_ready = sem("var_ready")
        sqrt_done = sem("sqrt_done")
        xn_ready = sem("xn_ready")
        xt_ready, xt_done, xrow_done, rows_split = (sem(n) for n in ("xt_ready", "xt_done", "xrow_done", "rows_split"))
        q_ready, qhi_done, qlo_done = (sem(n) for n in ("q_ready", "qhi_done", "qlo_done"))
        c_ready, ct_done = sem("c_ready"), sem("ct_done")
        r_ready, rmul_done, radd_done, rhi_done, rlo_done, rt_ready, rope_done = (
            sem(n) for n in ("r_ready", "rmul_done", "radd_done", "rhi_done", "rlo_done", "rt_ready", "rope_done"))
        k_ready, khi_done, klo_done = (sem(n) for n in ("k_ready", "khi_done", "klo_done"))
        v_ready, v_done = sem("v_ready"), sem("v_done")
        logit_done = sem("logit_done")
        gate_ready, gap_ready, gexp_done, comb_ready = (
            sem(n) for n in ("gate_ready", "gap_ready", "gexp_done", "comb_ready"))
        sel_ready = sem("sel_ready")
        rows_ready = sem("rows_ready")
        table_ready = sem("table_ready")
        zeros_ready = sem("zeros_ready")
        filled = sem("filled")
        scattered = sem("scattered")
        slot_in = [sem(f"slot_in{i}") for i in range(XIN)]
        wsc_done, whi_done, wlo_done = sem("wsc_done"), sem("whi_done"), sem("wlo_done")
        up_g, up_v = sem("up_g"), sem("up_v")
        b1_done = sem("b1_done")
        silu_done = sem("silu_done")
        hid_done = sem("hid_done")
        down_ready = sem("down_ready")
        y_done = sem("y_done")
        stored = sem("stored")
        gathered = [sem(f"gathered{i}") for i in range(YIN)]
        mixed = sem("mixed")
        acc_done = sem("acc_done")
        load = [sem(f"load{g}") for g in range(NG)]
        mrow = [[sem(f"mrow{g}_{c}") for c in range(CPB)] for g in range(NG)]
        mstore = [[sem(f"mstore{g}_{c}") for c in range(CPB)] for g in range(NG)]
        qk_store = [sem(f"qk_store{b}") for b in range(B)]
        ring_ready, ring_done = sem("ring_ready"), sem("ring_done")
        msplit_done = sem("msplit_done")
        s_ready, exp_done = sem("s_ready"), sem("exp_done")
        mask_done = sem("mask_done")
        pv_done = sem("pv_done")
        o_done = sem("o_done")
        out_sem = sem("out_sem")

        block = ctx.enter_context(nc.Block())

        @block.sync
        def _(sp):
            xv = x.rearrange("(c t p) d -> c p t d", p=PART, t=TPC)
            for c in range(NC):
                sp.dma_start(acc[:, c * TPC:(c + 1) * TPC, :], xv[c]).then_inc(ld_x[c], 16)
            for i in range(2):
                sp.dma_start(raw12[:, i, :], w12[i]).then_inc(ld_w12, 16)
            sp.dma_start(w3_sb[:, :], w3).then_inc(ld_w3, 16)
            sp.wait_ge(zeros_ready, 1)
            sp.dma_start(xbuf.rearrange("(q p) d -> p q d", p=PART),
                         zeros[:, :].unsqueeze(1).broadcast_to([PART, SLOTS * SH, 2 * D])).then_inc(filled, 16)

            def load_group(g):
                b, slot0 = g // GPB, G4 * (g % GPB)
                cols = slice(b * T, (b + 1) * T)

                def rot(rows, part, src):
                    sp.dma_start(stacks(slot0, (HROW + rows[0] * DR, HROW + rows[1] * DR), part),
                                 rope_s[src[0]:src[1], cols].unsqueeze(1).broadcast_to([src[1] - src[0], G4, T])
                                 ).then_inc(load[g], 16)
                rot((0, 2), 0, (0, 64))
                rot((2, 3), 0, (0, 32))
                rot((0, 1), 1, (64, 96))
                rot((1, 3), 1, (64, 128))
                if b == 0:
                    sp.dma_start(stacks(slot0, (QK_ROWS, ALL_ROWS), 1),
                                 kappa.unsqueeze(1).broadcast_to([2, G4, T])).then_inc(load[g], 16)
                heads = qkbuf[b, G4 * (g % GPB):G4 * (g % GPB + 1)].rearrange("j d t -> d j t")
                st = stack_a[:, :] if slot0 == 0 else stack_b[:, slot0 - G4:slot0]
                for r, which in ((0, QLO), (1, QHI)):
                    sp.dma_start(st[r * HD:(r + 1) * HD].rearrange("d j q t -> d j (q t)"),
                                 heads[:, :, which * T:(which + 2) * T]).then_inc(load[g], 16)
                for part, which in ((0, QHI), (1, KHI)):
                    sp.dma_start(st[2 * HD:3 * HD, :, part], heads[:, :, which * T:(which + 1) * T]
                                 ).then_inc(load[g], 16)

            def store_maxima(g, c):
                sp.wait_ge(ring_done, ring_at["mT", g, c] + 1)
                sp.dma_start(maxbuf[g, c].rearrange("s j (i t) -> (s j i) t", t=PART), max_t[:, c, :]
                             ).then_inc(mstore[g][c], 16)
                sp.wait_ge(mstore[g][c], 16)
                slot0 = G4 * (g % GPB)
                st = stack_a[:, :] if slot0 == 0 else stack_b[:, slot0 - G4:slot0]
                sp.dma_start(st[QK_ROWS:ALL_ROWS, :, 0, c * BANK:(c + 1) * BANK], maxbuf[g, c]
                             ).then_inc(mrow[g][c], 16)

            def load_slot(s):
                sp.dma_start(xin[:, s % XIN], xbuf[s * SLOT:(s + 1) * SLOT, :].rearrange("(h p) d -> p h d", p=PART)
                             ).then_inc(slot_in[s % XIN], 16)

            ov = out.rearrange("(c t p) d -> c p t d", p=PART, t=TPC)

            def store_out(b):
                for c in range(CPB):
                    n = b * CPB + c
                    sp.wait_ge(ring_done, ring_at["wo", b, c] + 1)
                    sp.wait_ge(mixed, TOPK * TPC * (n + 1))
                    sp.dma_start(ov[n], acc[:, n * TPC:(n + 1) * TPC, :]).then_inc(out_sem, 16)

            for b in range(B):
                for s in (qhi_done, qlo_done, khi_done, klo_done):
                    sp.wait_ge(s, CPB * (b + 1))
                sp.dma_start(qkbuf[b].rearrange("h d t -> (h d) t"), planes[b].rearrange("p k t -> p (k t)")
                             ).then_inc(qk_store[b], 16)
            sp.wait_ge(rope_done, B)
            sp.wait_ge(qk_store[0], 16)
            load_group(0)
            sp.wait_ge(v_ready, NC)
            sp.wait_ge(xn_ready, NT)
            store_maxima(0, 0)
            load_group(1)
            for n in range(NG * NCOL):
                if n == SCATTERED:
                    sp.wait_ge(scattered, 16 * TOPK * NT)
                    for s in range(XIN):
                        load_slot(s)
                if n == MID:
                    for s in range(0, SLOTS, 4):
                        sp.wait_ge(y_done, 2 + s + 4)
                        sp.dma_start(ybuf[s * SLOT:(s + 4) * SLOT, :].rearrange("(h p) d -> p h d", p=PART),
                                     ys[:, s:s + 4].rearrange("p s (h d) -> p (s h) d", d=D)).then_inc(stored, 16)
                if n == NG * NCOL - NCOL:
                    store_out(0)
                for item in slots[n]:
                    if item[0] == "mT":
                        store_maxima(*item[1:])
                        g = item[1] + 1
                        if item[2] == 0 and g < NG:
                            if g >= GPB:
                                sp.wait_ge(qk_store[1], 16)
                                sp.wait_ge(s_ready, G4 * NCOL * (g - GPB + 1))
                            load_group(g)
                    if item[0] == "turn" and item[1] + XIN < SLOTS:
                        sp.wait_ge(ring_ready, ring_at[item] + 1)
                        load_slot(item[1] + XIN)
            for b in range(1, B):
                store_out(b)
            sp.wait_ge(out_sem, 16 * NC)
            sp.wait_ge(filled, 16)
            sp.wait_ge(scattered, 16 * TOPK * NT)
            sp.wait_ge(stored, 16 * (SLOTS // 4))

        @block.gpsimd
        def _(pool):
            pool.memset(identf[:, :], 0.0).then_inc(pool_chain, 1)
            pool.memset(causal[:, :], 0.0).then_inc(pool_chain, 1)
            pool.wait_ge(pool_chain, 1)
            pool.affine_select(out=identf[:, :], in_=identf[:, :], compare_op=ALU.not_equal, fill=1.0, base=0,
                               pattern=[[-1, PART]], channel_multiplier=1).then_inc(pool_const, 1)
            pool.wait_ge(pool_const, 1)
            pool.tensor_copy(identh[:, :], identf[:, :]).then_inc(pool_const, 1)
            pool.tensor_copy(identb[:, :], identf[:, :]).then_inc(pool_const, 1)
            pool.memset(zeros[:, :], 0.0).then_inc(zeros_ready, 1)
            pool.wait_ge(amax_done, 3)
            pool.partition_all_reduce(amax_all[:, 0:3], amax[:, 0:3], PART, bass.bass_isa.ReduceOp.max
                                      ).then_inc(amax_red, 1)
            pool.wait_ge(pool_chain, 2)
            pool.affine_select(out=causal[:, :], in_=causal[:, :], compare_op=ALU.is_ge, fill=NEG, base=0,
                               pattern=[[-1, PART]], channel_multiplier=1).then_inc(pool_const, 1)
            pool.memset(v_aug[:, :, :, HD:HD + 1], 1.0).then_inc(pool_const, 1)
            pool.memset(ones_h[:, :], 1.0).then_inc(pool_chain, 1)
            pool.wait_ge(pool_chain, 3)
            pool.affine_select(out=before[:, :], in_=ones_h[:, :], compare_op=ALU.is_ge, fill=0.0, base=-1,
                               pattern=[[1, PART]], channel_multiplier=-1).then_inc(pool_const, 1)
            pool.wait_ge(xn_ready, NT)
            pool.wait_ge(xrow_done, 1)
            pool.tensor_tensor(x_rows[:, :, D:2 * D], xn[:, :, :], x_rows[:, :, 0:D], ALU.subtract
                               ).then_inc(rows_split, 1)

            pool.wait_ge(amax_done, 5)
            pool.partition_all_reduce(amax_all[:, 3:5], amax[:, 3:5], PART, bass.bass_isa.ReduceOp.max
                                      ).then_inc(amax_red, 1)

            def split_weights(i, half):
                cols = slice(half * E * FF // 2, (half + 1) * E * FF // 2)
                pool.wait_ge(whi_done, i + 1)
                pool.tensor_tensor(w_lo[:, i, cols], raw12[:, i, cols], w_hi[:, i, cols], ALU.subtract
                                   ).then_inc(wlo_done, 1)

            def scatter(m):
                k, t = m % TOPK, m // TOPK
                if m == 0:
                    pool.wait_ge(filled, 16)
                    pool.wait_ge(rows_ready, 1)
                    pool.wait_ge(rows_split, 1)
                pool.indirect_dma_start(xbuf, bass.IndirectOffsetOnAxis(rows_i[:, k * NT + t:k * NT + t + 1], 0),
                                        x_rows[:, t, :], None, bounds_check=SLOTS * SLOT - 1, oob_is_err=False
                                        ).then_inc(scattered, 16)

            def gather(m):
                k, t = m % TOPK, m // TOPK
                if m == 0:
                    pool.wait_ge(stored, 16 * (SLOTS // 4))
                if m >= YIN:
                    pool.wait_ge(mixed, m - YIN + 1)
                pool.indirect_dma_start(y_in[:, m % YIN, :], None, ybuf,
                                        bass.IndirectOffsetOnAxis(rows_i[:, k * NT + t:k * NT + t + 1], 0),
                                        bounds_check=SLOTS * SLOT - 1, oob_is_err=False
                                        ).then_inc(gathered[m % YIN], 16)

            for n in range(NG * NCOL):
                c, kt, at, diagonal = columns(0)[n % NCOL]
                if diagonal:
                    pool.wait_ge(exp_done, G4 * (n + 1))
                    p = probs[:, n % 3, :, at:at + PART]
                    pool.affine_select(out=p, in_=p, compare_op=ALU.is_ge, fill=0.0, base=0,
                                       pattern=[[0, G4], [1, PART]], channel_multiplier=-1
                                       ).then_inc(mask_done, 1)
                if 4 <= n < 8:
                    split_weights(*divmod(n - 4, 2))
                for m in SCATTERS.get(n, ()):
                    scatter(m)
                for m in GATHERS.get(n, ()):
                    gather(m)

        @block.scalar
        def _(act):
            act.dma_start(pack[:, :], wpack).then_inc(ld_pack, 16)
            act.dma_start(rope_c[:, :, :], rope).then_inc(ld_rope, 16)
            act.dma_start(b3_sb[:, :], b3).then_inc(ld_b3, 16)
            act.wait_ge(var_ready, 1)
            act.activation(ln[:, 1, :], ln[:, 0, :], ACT.Sqrt).then_inc(sqrt_done, 1)
            for c in range(NC):
                cols = slice(c * BANK, (c + 1) * BANK)
                act.wait_ge(xt_ready, c + 1)
                act.activation(x_t[:, cols], bank(c), ACT.Copy).then_inc(xt_done, 1)
            for c in range(NC):
                act.wait_ge(c_ready, c + 1)
                act.activation(c_t[:, c * BANK:(c + 1) * BANK], bank(c), ACT.Copy).then_inc(ct_done, 1)
            act.wait_ge(scales_ready, 1)
            for c in range(NC):
                act.wait_ge(q_ready, c + 1)
                act.activation(plane(QHI, c), bank(4 + c), ACT.Copy, scale=ALPHA).then_inc(qhi_done, 1)
            for c in range(NC):
                act.wait_ge(k_ready, c + 1)
                act.activation(plane(KHI, c), bank(c), ACT.Copy, scale=BETA).then_inc(khi_done, 1)
            for s in range(2):
                act.wait_ge(radd_done, s + 1)
                act.activation(rope_hl[:, :, 2 * s, :], rope_sum[:, s], ACT.Copy, scale=scales[:, s:s + 1]
                               ).then_inc(rhi_done, 1)
            for b in range(B):
                act.wait_ge(rt_ready, b + 1)
                act.activation(rope_s[:, b * T:(b + 1) * T], bank(4 + b).bitcast(F16), ACT.Copy
                               ).then_inc(rope_done, 1)
            act.activation(x_rows[:, :, 0:D], xn[:, :, :], ACT.Copy).then_inc(xrow_done, 1)
            for c in range(NC):
                act.wait_ge(v_ready, c + 1)
                act.activation(v_aug[:, c * TPC:(c + 1) * TPC, :, 0:HD],
                               bank(c).rearrange("p (t h d) -> p t h d", t=TPC, h=NH), ACT.Copy).then_inc(v_done, 1)
            act.wait_ge(gap_ready, 1)
            act.activation(rw[:, 1, :], rw[:, 0, :], ACT.Exp).then_inc(gexp_done, 1)

            def gates(s, k):
                act.wait_ge(up_g, s + 1)
                act.wait_ge(b1_done, s + 1)
                for j in range(FJ):
                    ins = act.activation(silu[:, k, j, :], bank(k, j * SLOT, (j + 1) * SLOT), ACT.Silu,
                                         bias=b1_e[:, k, j:j + 1], scale=IA1)
                ins.then_inc(silu_done, 1)

            def output_rows(q):
                act.wait_ge(pv_done, NCOL * (q // CPB) + (TPC, NCOL)[q % CPB])
                if q >= 2:
                    act.wait_ge(ring_ready, ring_at["oT", (q - 2) // CPB, q % CPB] + 1)
                act.activation(o_sb[:, q % 2, :], bank(6 + q % 2), ACT.Copy).then_inc(o_done, 1)

            act.wait_ge(scales_ready, 2)
            for i, a in enumerate((A1, A2)):
                act.activation(w_hi[:, i, :], raw12[:, i, :], ACT.Copy, scale=a).then_inc(wsc_done, 1)
                act.wait_ge(wsc_done, i + 1)
                act.activation(raw12[:, i, :], raw12[:, i, :], ACT.Copy, scale=a).then_inc(whi_done, 1)
            act.wait_ge(rows_split, 1)
            act.wait_ge(gate_ready, 1)
            u = 0
            for g in range(NG):
                if g * NCOL == MID:
                    for k in range(2):
                        gates(k, k)
                    with act.Fori(1, SLOTS // 2) as i:
                        for k in range(2):
                            gates(2 * i + k, k)
                for k, (c, kt, at, _) in enumerate(columns(g)):
                    n = g * NCOL + k
                    for j in range(G4):
                        act.wait_ge(s_ready, u + 1)
                        if n >= 3 and j == 0:
                            act.wait_ge(pv_done, n - 2)
                        act.activation(probs[:, n % 3, j, at:BANK], bank(sbank[u], at), ACT.Exp, scale=float(EXP_SCALE)
                                       ).then_inc(exp_done, 1)
                        u += 1
                    if k == TPC:
                        output_rows(CPB * g)
                    if k == 0 and g:
                        output_rows(CPB * g - 1)
            output_rows(CPB * NG - 1)

        @block.tensor
        def _(pe):
            pe.wait_ge(pool_const, 3)
            for t in range(NT):
                pe.wait_ge(xn_ready, t + 1)
                mm = pe.transpose(bank(t // TPC, t % TPC * PART, t % TPC * PART + PART), xn[:, t, :], identf[:, :])
                if t % TPC == TPC - 1:
                    mm.then_inc(xt_ready, 1)
            pe.wait_ge(ld_pack, 16)
            for c in range(NC):
                pe.wait_ge(xt_done, c + 1)
                pe.matmul(bank(c), w("wkv"), x_t[:, c * BANK:(c + 1) * BANK], start=True, stop=True
                          ).then_inc(c_ready, 1)
            for c in range(NC):
                pe.matmul(bank(4 + c), w("wq"), x_t[:, c * BANK:(c + 1) * BANK], start=True, stop=True
                          ).then_inc(q_ready, 1)
            for c in range(NC):
                pe.wait_ge(ct_done, c + 1)
                pe.matmul(bank(c), w("wk"), c_t[:, c * BANK:(c + 1) * BANK], start=True, stop=True
                          ).then_inc(k_ready, 1)

            def rotary(s, source, weights):
                for b in range(B):
                    pe.wait_ge(qhi_done, 2 * s + b + 1)
                    pe.wait_ge(qlo_done, 2 * s + b + 1)
                    for t in range(KT):
                        at = (b * KT + t) * PART
                        mm = pe.matmul(bank(4 + 2 * s + b, t * 2 * DR, (t + 1) * 2 * DR), source[:, at:at + PART],
                                       weights, start=True, stop=True)
                    mm.then_inc(r_ready, 1)

            rotary(0, x_t, w("wqr"))
            rotary(1, c_t, w("wkr"))
            for c in range(NC):
                pe.wait_ge(khi_done, c + 1)
                pe.wait_ge(klo_done, c + 1)
                for t in range(TPC):
                    at = (c * TPC + t) * PART
                    mm = pe.matmul(bank(c, t * PART, (t + 1) * PART), c_t[:, at:at + PART], w("wv"),
                                   start=True, stop=True)
                mm.then_inc(v_ready, 1)
            pe.wait_ge(rhi_done, 2)
            pe.wait_ge(rlo_done, 2)
            for b in range(B):
                for t in range(KT):
                    mm = pe.transpose(bank(4 + b, t * PART // 2, (t + 1) * PART // 2).bitcast(F16),
                                      rope_hl[:, b * KT + t].rearrange("p k d -> p (k d)"), identh[:, :])
                mm.then_inc(rt_ready, 1)
            for t in range(NT):
                mm = pe.matmul(bank(6, t * E, (t + 1) * E), x_t[:, t * PART:(t + 1) * PART], w("wg"),
                               start=True, stop=True)
            mm.then_inc(gate_ready, 1)
            pe.wait_ge(v_done, NC)
            pe.wait_ge(rope_done, B)
            pe.wait_ge(pool_const, 6)
            pe.wait_ge(logit_done, 1)

            def up(s, k, e):
                for i, ready in enumerate((up_g, up_v)):
                    for j in range(FJ):
                        dst = bank(2 * i + k, j * SLOT, (j + 1) * SLOT)
                        hi = w_hi[:, i, bass.ds(e + j * PART, PART)]
                        lo = w_lo[:, i, bass.ds(e + j * PART, PART)]
                        x_hi, x_lo = (xs[:, s, a * SLOT:(a + 1) * SLOT] for a in range(2))
                        pe.matmul(dst, hi, x_hi, start=True, stop=False)
                        pe.matmul(dst, hi, x_lo, start=False, stop=False)
                        mm = pe.matmul(dst, lo, x_hi, start=False, stop=True)
                    mm.then_inc(ready, 1)

            def down(k, e):
                parts = [w3_sb[:, bass.ds(e + j * D, D)] for j in range(FJ)]
                for h in range(SH):
                    for j in range(FJ):
                        mm = pe.matmul(bank(4 + k, h * D, (h + 1) * D), hid[:, k, j, h * PART:(h + 1) * PART],
                                       parts[j], start=(j == 0), stop=(j == FJ - 1))
                mm.then_inc(down_ready, 1)

            def experts_of(s, n):
                _, values = nc.values_load_multi_w_load_instructions(
                    etab[0:1, bass.ds(s, n)], engines=[mybir.EngineType.PE], min_val=0, max_val=(E - 1) * FF,
                    skip_runtime_bounds_check_because="DVE has clamped the expert to E - 1")
                return values

            def experts():
                pe.sem_inc(down_ready, 2)
                pe.wait_ge(ring_done, mid_ring)
                pe.wait_ge(exp_done, G4 * MID)
                pe.wait_ge(ld_w3, 16)
                pe.wait_ge(wlo_done, 4)
                pe.wait_ge(table_ready, 1)
                es = experts_of(0, 2)
                for s in range(2):
                    up(s, s, es[s])
                with pe.Fori(1, SLOTS // 2) as i:
                    es = experts_of(2 * i - 2, 4)
                    for k in range(2):
                        s = 2 * i + k
                        pe.wait_ge(hid_done, s - 1)
                        up(s, k, es[2 + k])
                        pe.wait_ge(y_done, s - 1)
                        down(k, es[k])
                es = experts_of(SLOTS - 2, 2)
                for k in range(2):
                    pe.wait_ge(hid_done, SLOTS - 1 + k)
                    pe.wait_ge(y_done, SLOTS - 1 + k)
                    down(k, es[k])
                pe.wait_ge(y_done, 2 + SLOTS)

            def ring_job(item):
                r = ring_at[item]
                kind = item[0]
                b0 = ring_bank(r)
                if r >= 2:
                    pe.wait_ge(ring_done, r - 1 if r < wide_ring else r)
                if kind == "max1":
                    _, g, j, i = item
                    slot = G4 * (g % GPB) + j
                    q = stack(slot, (0, QK_ROWS), 0, i * PART, (i + 1) * PART)
                    end = (i + 1) * PART
                    pe.matmul(bank(b0), q, stack(slot, (0, QK_ROWS), 1, 0, BANK), start=True, stop=True)
                    pe.matmul(bank(b0 + 1, 0, end - BANK), q, stack(slot, (0, QK_ROWS), 1, BANK, end),
                              start=True, stop=False)
                    mm = pe.matmul(bank(b0 + 1, end - BANK - PART, end - BANK), identb[:, :], causal[:, :],
                                   start=False, stop=True)
                elif kind == "max2":
                    _, g, j, i = item
                    end = (i + 1) * PART
                    for k in range(2):
                        slot = G4 * (g % GPB) + j + k
                        pe.matmul(bank(b0 + k, 0, end), stack(slot, (0, QK_ROWS), 0, i * PART, end),
                                  stack(slot, (0, QK_ROWS), 1, 0, end), start=True, stop=False)
                        mm = pe.matmul(bank(b0 + k, end - PART, end), identb[:, :], causal[:, :],
                                       start=False, stop=True)
                elif kind == "mT":
                    g = item[1]
                    pe.wait_ge(msplit_done, 2 * (CPB * g + item[2] + 1))
                    mm = pe.transpose(bank(b0, 0, PART // 2, p1=2 * G4 * TPC).bitcast(F16),
                                      max_s[:, g % 2, item[2]].rearrange("p s j i -> p (s j i)"), identh[:, :])
                elif kind == "oT":
                    q = item[1] * CPB + item[2]
                    pe.wait_ge(o_done, q + 1)
                    for t in range(TPC):
                        mm = pe.transpose(bank(b0, t * PART, (t + 1) * PART),
                                          o_sb[:, q % 2, t * PART:(t + 1) * PART], identf[:, :])
                elif kind == "aT":
                    _, b, c = item
                    pe.wait_ge(ring_done, ring_at["oT", GPB * (b + 1) - 1, c] + 1)
                    for t in range(TPC):
                        mm = pe.transpose(bank(b0, t * PART, (t + 1) * PART), attn[:, c * TPC + t, :],
                                          identf[:, :])
                elif kind == "cT":
                    _, b, c = item
                    pe.wait_ge(comb_ready, 1)
                    for t in range(TPC):
                        mm = pe.transpose(bank(b0, t * PART, (t + 1) * PART, p1=E),
                                          comb[:, b * KT + c * TPC + t, :], identf[:, :])
                elif kind == "count":
                    pe.wait_ge(sel_ready, 1)
                    pe.wait_ge(pool_const, 6)
                    mm = pe.matmul(bank(b0, 0, NT * E), before[:, :], sel.rearrange("p t e -> p (t e)"),
                                   start=True, stop=False)
                    for t in range(NT - 1):
                        pe.matmul(bank(b0, (t + 1) * E, NT * E), ones_h[:, :],
                                  sel[:, t:t + 1, :].broadcast_to([PART, NT - 1 - t, E]),
                                  start=False, stop=(t == NT - 2))
                    for t in range(NT):
                        mm = pe.matmul(bank(b0 + 1, 0, E), ones_h[:, :], sel[:, t, :], start=(t == 0),
                                       stop=(t == NT - 1))
                elif kind == "turn":
                    s = item[1]
                    pe.wait_ge(slot_in[s % XIN], 16 * (s // XIN + 1))
                    for h in range(SH):
                        for a in range(2):
                            at = (a * SLOT + h * PART) // 2
                            mm = pe.transpose(bank(b0, at, at + PART // 2).bitcast(F16),
                                              xin[:, s % XIN, h, a * D:(a + 1) * D], identh[:, :])
                else:
                    _, b, c = item
                    pe.wait_ge(ring_done, max(ring_at["aT", b, c], ring_at["cT", b, c]) + 1)
                    for t in range(TPC):
                        tile = b * KT + c * TPC + t
                        pe.matmul(bank(b0, t * PART, (t + 1) * PART), attn_t[:, c, t * PART:(t + 1) * PART],
                                  w("wo"), start=True, stop=False)
                        mm = pe.matmul(bank(b0, t * PART, (t + 1) * PART),
                                       comb_t[:, t * PART:(t + 1) * PART], b3_sb[:, :],
                                       start=False, stop=True)
                mm.then_inc(ring_ready, 1)

            def prob_values(n):
                g, k = divmod(n, NCOL)
                c, kt, at, diagonal = columns(g)[k]
                pe.wait_ge(exp_done, G4 * (n + 1))
                if diagonal:
                    pe.wait_ge(mask_done, masks[n])
                q = CPB * g + c
                if kt == 0 and q >= 2:
                    pe.wait_ge(o_done, q - 1)
                tile = KT * (g // GPB) + kt
                for j in range(G4):
                    mm = pe.matmul(bank(6 + q % 2, at, BANK, p0=32 * j, p1=32 * j + HD + 1),
                                   v_aug[:, tile, G4 * (g % GPB) + j, :], probs[:, n % 3, j, at:BANK],
                                   start=(kt == 0), stop=(kt == TPC * (c + 1) - 1))
                mm.then_inc(pv_done, 1)

            masks, found = {}, 0
            for n in range(NG * NCOL):
                if columns(0)[n % NCOL][3]:
                    found += 1
                    masks[n] = found

            pe.wait_ge(ld_b3, 16)
            loads = {}

            def stacks_loaded(g):
                if g not in loads:
                    loads[g] = True
                    pe.wait_ge(load[g], 16 * (4 + (g < GPB) + 4))

            def run_ring(items):
                for item in items:
                    if item[0] in ("max1", "max2"):
                        stacks_loaded(item[1])
                    ring_job(item)

            run_ring(first)
            u = 0
            for g in range(NG):
                if g * NCOL == MID:
                    prob_values(MID - 1)
                    experts()
                for k, (c, kt, at, _) in enumerate(columns(g)):
                    n = g * NCOL + k
                    ring = slots[n]
                    half = (len(ring) + 1) // 2
                    if kt == 0:
                        pe.wait_ge(mrow[g][c], 16)
                    for j in range(G4):
                        slot = G4 * (g % GPB) + j
                        before_u = [v for v in range(u) if sbank[v] == sbank[u]]
                        if before_u:
                            pe.wait_ge(exp_done, before_u[-1] + 1)
                        if sbank[u] < 4 and len(before_u) == 0:
                            pe.wait_ge(ring_done, wide_ring)
                        pe.matmul(bank(sbank[u], at), stack(slot, (0, ALL_ROWS), 1, kt * PART, (kt + 1) * PART),
                                  stack(slot, (0, ALL_ROWS), 0, c * BANK + at, (c + 1) * BANK),
                                  start=True, stop=True).then_inc(s_ready, 1)
                        u += 1
                        if j == 1:
                            run_ring(ring[:half])
                        if j == 2 and n and n != MID:
                            prob_values(n - 1)
                    run_ring(ring[half:])
            prob_values(NG * NCOL - 1)
            run_ring(tail)

        @block.vector
        def _(dve):
            chained = [0]

            def step(ins):
                chained[0] += 1
                return ins.then_inc(dve_chain, 1)

            def settle():
                dve.wait_ge(dve_chain, chained[0])

            for c in range(NC):
                dve.wait_ge(ld_x[c], 16)
                for t in range(c * TPC, (c + 1) * TPC):
                    step(dve.bn_stats(stats[:, t, :], acc[:, t, :]))
                if c == 0:
                    dve.wait_ge(ld_pack, 16)
                    for n, (a, b) in enumerate((("wq", "wqr"), ("wkv", "wkv"), ("wk", "wkr"))):
                        dve.tensor_reduce(amax[:, n:n + 1], pack[:, PACK[a][0]:PACK[b][1]], AX.X, ALU.max,
                                          apply_absolute_value=True).then_inc(amax_done, 1)
            settle()
            for t in range(NT):
                step(dve.bn_aggr(mv[:, t, :], stats[:, t, :]))
            settle()
            dve.tensor_scalar(ln[:, 0, :], mv[:, :, 1], EPS, None, ALU.add).then_inc(var_ready, 1)
            dve.wait_ge(sqrt_done, 1)
            step(dve.reciprocal(ln[:, 2, :], ln[:, 1, :]))
            settle()
            step(dve.tensor_tensor(ln[:, 3, :], ln[:, 0, :], ln[:, 2, :], ALU.mult))
            settle()
            step(dve.tensor_tensor(ln[:, 4, :], ln[:, 3, :], ln[:, 1, :], ALU.add))
            settle()
            step(dve.tensor_scalar(ln[:, 2, :], ln[:, 4, :], 0.5, None, ALU.mult))
            settle()
            step(dve.reciprocal(ln[:, 5, :], ln[:, 2, :]))
            settle()
            for t in range(NT):
                dve.tensor_scalar(xn[:, t, :], acc[:, t, :], mv[:, t, 0:1], ln[:, 5, t:t + 1], ALU.subtract, ALU.mult
                                  ).then_inc(xn_ready, 1)
            def powers(a, b):
                step(dve.tensor_scalar(pow2[:, a:b], amax_all[:, a:b], 2.0 ** -30, None, ALU.max))
                settle()
                step(dve.tensor_scalar(pow2[:, a:b].bitcast(I32), pow2[:, a:b].bitcast(I32), 0x7F800000, None,
                                       ALU.bitwise_and))
                settle()
                step(dve.reciprocal(ipow[:, a:b], pow2[:, a:b]))
                settle()
            dve.wait_ge(amax_red, 1)
            powers(0, 3)
            step(dve.tensor_scalar(TMP, pow2[:, 0:1], pow2[:, 1:2], pow2[:, 2:3], ALU.mult, ALU.mult))
            settle()
            step(dve.tensor_scalar(TMP.bitcast(I32), TMP.bitcast(I32), 1, 0x7F800000,
                                   ALU.logical_shift_right, ALU.bitwise_and))
            settle()
            step(dve.tensor_scalar(TMP, TMP, 2.0 ** 64, None, ALU.mult))
            settle()
            step(dve.tensor_scalar(ALPHA, ipow[:, 0:1], TMP, 2.0 ** 4, ALU.mult, ALU.mult))
            settle()
            step(dve.tensor_scalar(TMP2, ALPHA, 1.0 / QK_SCALE, None, ALU.mult))
            settle()
            step(dve.reciprocal(BETA, TMP2))
            settle()
            dve.sem_inc(scales_ready, 1)

            def low(plane_lo, plane_hi, b0, scale, hi_done, done):
                for c in range(NC):
                    dve.wait_ge(hi_done, c + 1)
                    dve.scalar_tensor_tensor(out=plane(plane_lo, c), in0=bank(b0 + c), scalar=scale,
                                             in1=plane(plane_hi, c), op0=ALU.mult, op1=ALU.subtract
                                             ).then_inc(done, 1)

            def rotate(s):
                for b in range(B):
                    dve.wait_ge(r_ready, 2 * s + b + 1)
                    dve.tensor_tensor(rope_m[:, s, b * KT:(b + 1) * KT],
                                      bank(4 + 2 * s + b).rearrange("p (t d) -> p t d", d=2 * DR),
                                      rope_c[:, :, :], ALU.mult).then_inc(rmul_done, 1)
                dve.wait_ge(rmul_done, 2 * s + 2)
                dve.tensor_tensor(rope_sum[:, s], rope_m[:, s, :, 0:DR], rope_m[:, s, :, DR:2 * DR], ALU.add
                                  ).then_inc(radd_done, 1)

            low(QLO, QHI, 4, ALPHA, qhi_done, qlo_done)
            low(KLO, KHI, 0, BETA, khi_done, klo_done)
            dve.wait_ge(ld_rope, 16)
            for s in range(2):
                rotate(s)
            for s in range(2):
                dve.wait_ge(rhi_done, s + 1)
                dve.scalar_tensor_tensor(out=rope_hl[:, :, 2 * s + 1, :], in0=rope_sum[:, s],
                                         scalar=scales[:, s:s + 1], in1=rope_hl[:, :, 2 * s, :],
                                         op0=ALU.mult, op1=ALU.subtract).then_inc(rlo_done, 1)
            dve.wait_ge(gate_ready, 1)
            dve.tensor_copy(logit[:, :, :], bank(6, 0, NT * E).rearrange("p (t e) -> p t e", e=E)
                            ).then_inc(logit_done, 1)
            dve.wait_ge(logit_done, 1)
            for t in range(NT):
                step(dve.max(top[:, t, :], logit[:, t, :]))
            settle()
            dve.tensor_tensor(rw[:, 0, :], top[:, :, 1], top[:, :, 0], ALU.subtract).then_inc(gap_ready, 1)
            dve.wait_ge(ld_w12, 32)
            for i in range(2):
                dve.tensor_reduce(amax[:, 3 + i:4 + i], raw12[:, i, :], AX.X, ALU.max,
                                  apply_absolute_value=True).then_inc(amax_done, 1)
            dve.wait_ge(amax_red, 2)
            powers(3, 5)
            for n, (a, ia) in enumerate(((A1, IA1), (A2, IA2))):
                step(dve.tensor_scalar(a, ipow[:, 3 + n:4 + n], 2.0 ** 13, None, ALU.mult))
                step(dve.tensor_scalar(ia, pow2[:, 3 + n:4 + n], 2.0 ** -13, None, ALU.mult))
            settle()
            dve.sem_inc(scales_ready, 1)
            step(dve.tensor_scalar(b2_s[:, :], w("b2"), A2, None, ALU.mult))

            iota = w("iota")

            def along(a, n):
                return a.unsqueeze(1).broadcast_to([PART, n, a.shape[1]])

            def across(a, n):
                return a.unsqueeze(2).broadcast_to([PART, a.shape[1], n])

            def route_choices():
                for t in range(NT):
                    step(dve.max_index(topi[:, t, :], top[:, t, :], logit[:, t, :]))
                settle()
                step(dve.tensor_copy(topf[:, :, :], topi[:, :, :]))
                settle()
                for n in range(TOPK):
                    step(dve.tensor_tensor(eq[:, n], across(topf[:, :, n], E), along(iota[:, 0:E], NT), ALU.is_equal))
                settle()
                dve.tensor_tensor(sel[:, :, :], eq[:, 0], eq[:, 1], ALU.add).then_inc(sel_ready, 1)

            def route_rows():
                total, slots_of, end, start, limit = (per_e[:, i] for i in range(5))
                step(dve.tensor_scalar(limit, iota[:, 0:E], float(SLOT), None, ALU.mult))
                step(dve.tensor_tensor(small[:, 1], along(iota[:, 0:E], E), across(iota[:, 0:E], E), ALU.is_le))
                settle()
                step(dve.tensor_tensor(small[:, 0], across(total, E), along(limit, E), ALU.is_gt))
                settle()
                step(dve.tensor_reduce(slots_of, small[:, 0], AX.X, ALU.add))
                settle()
                step(dve.tensor_tensor(small[:, 0], small[:, 1], along(slots_of, E), ALU.mult))
                settle()
                step(dve.tensor_reduce(end, small[:, 0], AX.X, ALU.add))
                settle()
                step(dve.tensor_tensor(start, end, slots_of, ALU.subtract))
                settle()
                step(dve.scalar_tensor_tensor(out=pos[:, :, :], in0=along(start, NT), scalar=float(SLOT),
                                              in1=pos[:, :, :], op0=ALU.mult, op1=ALU.add))
                settle()
                for n in range(TOPK):
                    step(dve.tensor_tensor(picked[:, n], eq[:, n], pos[:, :, :], ALU.mult))
                settle()
                step(dve.tensor_reduce(rows_f[:, :, :], picked[:, :, :, :], AX.X, ALU.add))
                settle()
                dve.tensor_copy(rows_i[:, :], rows_f.rearrange("p k t -> p (k t)")).then_inc(rows_ready, 1)

            def route_table():
                end = per_e[:, 2]
                step(dve.tensor_tensor(slot_e[:, 0], along(end, TAB), across(iota[:, 0:TAB], E), ALU.is_le))
                settle()
                step(dve.tensor_reduce(slot_f[:, 0], slot_e[:, 0], AX.X, ALU.add))
                settle()
                step(dve.tensor_scalar(slot_f[:, 1], slot_f[:, 0], float(E - 1), None, ALU.min))
                settle()
                step(dve.tensor_scalar(etab[:, :], slot_f[:, 1], float(FF), None, ALU.mult))
                step(dve.tensor_tensor(slot_e[:, 1], along(iota[:, 0:E], TAB), across(slot_f[:, 1], E), ALU.is_equal))
                settle()

            def route_biases(biases, table):
                for j in range(FJ):
                    step(dve.tensor_tensor(slot_e[:, 0], slot_e[:, 1],
                                           along(biases.rearrange("p (e j) -> p j e", j=FJ)[:, j], TAB), ALU.mult))
                    settle()
                    step(dve.tensor_reduce(table[:, j], slot_e[:, 0], AX.X, ALU.add))
                    settle()

            def route_weights():
                dve.wait_ge(gexp_done, 1)
                step(dve.tensor_scalar(rw[:, 2, :], rw[:, 1, :], 1.0, None, ALU.add))
                settle()
                step(dve.reciprocal(rw[:, 3, :], rw[:, 2, :]))
                settle()
                step(dve.tensor_tensor(rw[:, 2, :], rw[:, 1, :], rw[:, 3, :], ALU.mult))
                settle()
                for n in range(TOPK):
                    step(dve.tensor_scalar(wmix[:, n], rw[:, 3 - n, :], IA2, None, ALU.mult))
                    step(dve.tensor_tensor(picked[:, n], eq[:, n], across(rw[:, 3 - n, :], E), ALU.mult))
                settle()
                dve.tensor_tensor(comb[:, :, :], picked[:, 0], picked[:, 1], ALU.add).then_inc(comb_ready, 1)

            def routing(n):
                if n == 0:
                    route_choices()
                elif n == 3:
                    route_rows()
                elif n == 4:
                    route_table()
                elif n == 5:
                    route_biases(w("b1"), b1_t)
                elif n == 6:
                    route_biases(b2_s[:, :], b2_t)
                    dve.sem_inc(table_ready, 1)
                elif n == 7:
                    route_weights()

            def bias(s, k):
                dve.tensor_scalar(b1_e[:, k, :], b1_t[:, :, s], 1.0, None, ALU.mult).then_inc(b1_done, 1)

            def hidden(s, k):
                dve.wait_ge(silu_done, s + 1)
                dve.wait_ge(up_v, s + 1)
                dve.wait_ge(down_ready, s + 1)
                for j in range(FJ):
                    ins = dve.scalar_tensor_tensor(out=hid[:, k, j, :], in0=bank(2 + k, j * SLOT, (j + 1) * SLOT),
                                                   scalar=b2_t[:, j, bass.ds(s, 1)], in1=silu[:, k, j, :],
                                                   op0=ALU.add, op1=ALU.mult)
                ins.then_inc(hid_done, 1)

            def output(s, k):
                dve.wait_ge(down_ready, 2 + s + 1)
                dve.tensor_copy(ys[:, s, :], bank(4 + k, 0, SH * D)).then_inc(y_done, 1)

            def experts():
                dve.sem_inc(y_done, 2)
                for k in range(2):
                    bias(slice(k, k + 1), k)
                for k in range(2):
                    hidden(k, k)
                    bias(slice(k + 2, k + 3), k)
                with dve.Fori(1, SLOTS // 2) as i:
                    for k in range(2):
                        hidden(2 * i + k, k)
                        bias(bass.ds(2 * i + k + 2, 1), k)
                        output(2 * i + k - 2, k)
                for k in range(2):
                    output(SLOTS - 2 + k, k)

            sums = [0]

            def into_acc(ins):
                sums[0] += 1
                ins.then_inc(acc_done, 1)

            def mix(m):
                k, t = m % TOPK, m // TOPK
                dve.wait_ge(gathered[m % YIN], 16 * (m // YIN + 1))
                if sums[0]:
                    dve.wait_ge(acc_done, sums[0])
                into_acc(dve.scalar_tensor_tensor(out=acc[:, t, :], in0=y_in[:, m % YIN, :], scalar=wmix[:, k, t:t + 1],
                                                  in1=acc[:, t, :], op0=ALU.mult, op1=ALU.add))
                dve.sem_inc(mixed, 1)

            def ring_result(item):
                r = ring_at[item]
                kind = item[0]
                b0 = ring_bank(r)
                dve.wait_ge(ring_ready, r + 1)
                if kind == "max1":
                    _, g, j, i = item
                    ins = dve.tensor_reduce(maxima[:, g % 2, j, i:i + 1],
                                            ps[:, b0 * BANK:b0 * BANK + (i + 1) * PART], AX.X, ALU.max)
                elif kind == "max2":
                    _, g, j, i = item
                    pair = ps[:, b0 * BANK:(b0 + 2) * BANK].rearrange("p (k n) -> p k n", k=2)
                    ins = dve.tensor_reduce(maxima[:, g % 2, j:j + 2, i], pair[:, :, 0:(i + 1) * PART], AX.X, ALU.max)
                elif kind == "mT":
                    g = item[1]
                    c = item[2]
                    if g >= 1:
                        dve.wait_ge(mstore[g - 1][c], 16)
                    ins = dve.tensor_copy(max_t[:, c, :], bank(b0, 0, PART // 2, p1=2 * G4 * TPC).bitcast(F16))
                elif kind == "oT":
                    _, g, c = item
                    q = g * CPB + c
                    o = bank(b0).rearrange("p (t j d) -> p t j d", t=TPC, j=G4)
                    step(dve.reciprocal(rden[:, q % 2], o[:, :, :, HD]))
                    settle()
                    h0 = G4 * HD * (g % GPB)
                    dst = attn[:, c * TPC:(c + 1) * TPC, h0:h0 + G4 * HD]
                    ins = dve.tensor_tensor(dst.rearrange("p t (j d) -> p t j d", j=G4), o[:, :, :, 0:HD],
                                            rden[:, q % 2].unsqueeze(3).broadcast_to([PART, TPC, G4, HD]), ALU.mult)
                elif kind == "aT":
                    _, b, c = item
                    ins = dve.tensor_copy(attn_t[:, c, :], bank(b0))
                elif kind == "cT":
                    _, b, c = item
                    ins = dve.tensor_copy(comb_t[:, :], bank(b0, p1=E))
                elif kind == "count":
                    dve.tensor_copy(pos[:, :, :], bank(b0, 0, NT * E).rearrange("p (t e) -> p t e", e=E))
                    ins = dve.tensor_copy(per_e[:, 0], bank(b0 + 1, 0, E))
                elif kind == "turn":
                    dve.wait_ge(wlo_done, 4)
                    ins = dve.tensor_copy(xs[:, item[1], :], bank(b0, 0, SLOT).bitcast(F16))
                else:
                    _, b, c = item
                    tiles = slice(b * KT + c * TPC, b * KT + (c + 1) * TPC)
                    if sums[0]:
                        dve.wait_ge(acc_done, sums[0])
                    ins = dve.tensor_tensor(acc[:, tiles, :], acc[:, tiles, :],
                                            bank(b0).rearrange("p (t d) -> p t d", t=TPC), ALU.add)
                ins.then_inc(ring_done, 1)
                if kind in ("wo", "count"):
                    dve.wait_ge(ring_done, r + 1)
                if kind in ("max1", "max2") and item == max_items(item[1], kind == "max1")[-1]:
                    g, c = item[1], int(kind == "max1")
                    dve.wait_ge(ring_done, r + 1)
                    m = maxima[:, g % 2, :, c * TPC:(c + 1) * TPC]
                    split = 2 * (CPB * g + c)
                    if g >= 2:
                        dve.wait_ge(ring_ready, ring_at["mT", g - 2, c] + 1)
                    dve.tensor_scalar(max_s[:, g % 2, c, 0], m, -1.0 / KAPPA, None, ALU.mult).then_inc(msplit_done, 1)
                    dve.wait_ge(msplit_done, split + 1)
                    dve.scalar_tensor_tensor(out=max_s[:, g % 2, c, 1], in0=m, scalar=-1.0 / KAPPA,
                                             in1=max_s[:, g % 2, c, 0], op0=ALU.mult, op1=ALU.subtract
                                             ).then_inc(msplit_done, 1)
                    dve.wait_ge(msplit_done, split + 2)

            for item in first:
                ring_result(item)
            for n in range(NG * NCOL):
                if n == MID:
                    experts()
                for item in slots[n]:
                    ring_result(item)
                routing(n)
                for m in GATHERS.get(n - 4, ()):
                    mix(m)
            for item in tail:
                ring_result(item)


def kernel(**inputs):
    import concourse.bacc as bacc
    from concourse.bass_utils import run_bass_kernel_spmd

    a = {k: np.asarray(v) for k, v in inputs.items()}
    h = DR // 2

    def both(wr):
        return np.concatenate([wr, wr[:, h:], wr[:, :h]], axis=1)

    def by_half(b):
        return b.reshape(E, FJ, PART).transpose(2, 0, 1).reshape(PART, E * FJ)

    f32 = np.float32
    freq = (f32(1.0) / np.power(f32(10000.0), np.arange(0, DR, 2, dtype=f32) / f32(DR))).astype(f32)
    angle = np.outer(np.arange(T, dtype=f32), freq).astype(f32)
    cos, sin = np.cos(angle), np.sin(angle)
    pack = np.concatenate([
        a["L0_attn_W_q"], both(a["L0_attn_W_q_rope"]), a["L0_attn_W_kv_down"], a["L0_attn_W_k_up"],
        both(a["L0_attn_W_k_rope"]), a["L0_attn_W_v_up"], a["L0_attn_W_o"], a["L0_ffn_Wg"].T,
        by_half(a["L0_ffn_b1"]), by_half(a["L0_ffn_b2"]),
        np.broadcast_to(np.arange(32, dtype=f32), (PART, 32))], axis=1)
    arrays = {
        "x": a["L0_attn_x"].reshape(TOK, D),
        "wpack": pack,
        "w12": np.stack([a["L0_ffn_W1"].transpose(2, 0, 1).reshape(D, E * FF),
                         a["L0_ffn_W2"].transpose(2, 0, 1).reshape(D, E * FF)]),
        "w3": a["L0_ffn_W3"].reshape(E, D, FJ, PART).transpose(3, 0, 2, 1).reshape(PART, E * FJ * D),
        "b3": a["L0_ffn_b3"],
        "rope": np.concatenate([cos, cos, -sin, sin], axis=1).reshape(KT, PART, 2 * DR).transpose(1, 0, 2),
        "kappa": np.full((2, T), KAPPA, np.float16),
    }
    arrays = {k: np.ascontiguousarray(v) for k, v in arrays.items()}
    nc = bacc.Bacc("TRN2", target_bir_lowering=False, num_devices=1)
    args = [nc.dram_tensor(k, v.shape, mybir.dt.from_np(v.dtype), kind="ExternalInput").ap()
            for k, v in arrays.items()]
    out = nc.dram_tensor("out", (TOK, D), F32, kind="ExternalOutput").ap()
    build(nc, *args, out)
    r = run_bass_kernel_spmd(nc, [arrays], core_ids=[0])
    return r.results[0]["out"].reshape(B, T, D)
```

```python
from contextlib import ExitStack

import numpy as np
import concourse.bass as bass
from concourse import mybir

F32 = mybir.dt.float32
F16 = mybir.dt.float16
BF16 = mybir.dt.bfloat16
I32 = mybir.dt.int32
U32 = mybir.dt.uint32
ALU = mybir.AluOpType
ACT = mybir.ActivationFunctionType
AX = mybir.AxisListType

PART = 128
BANK = 512
B, T, D = 2, 1024, 128
NH, HD, DR = 16, 8, 32
E, FF = 8, 256
TOK = B * T
NT = TOK // PART
NC = TOK // BANK
TPC = BANK // PART
FJ = FF // PART
G4 = 4
GPB = NH // G4
NG = B * GPB
KT = T // PART
CPB = T // BANK
EPS = 1e-5
KAPPA = 2.0 ** 15
QK_SCALE = 2.0 ** 8
EXP_SCALE = np.float32(1.0) / np.sqrt(np.float32(HD + DR)) / np.float32(QK_SCALE)
NEG = -1e30
HROW, RROW = 3 * HD, 3 * DR
QK_ROWS = HROW + RROW
ALL_ROWS = QK_ROWS + 2

PACK = {}
_at = 0
for _name, _n in (("wq", D), ("wqr", 2 * DR), ("wkv", D), ("wk", D), ("wkr", 2 * DR), ("wv", D), ("wo", D),
                  ("wg", E), ("b1", E * FJ), ("b2", E * FJ), ("iota", 32)):
    PACK[_name] = (_at, _at + _n)
    _at += _n
PACK_COLS = _at

QLO, KHI, QHI, KLO = range(4)

TOPK = 2
SLOT = 2 * PART
SH = SLOT // PART
SLOTS = 2 * -(-(TOK * TOPK // SLOT + E - 1) // 2)
TAB = SLOTS + 2
assert TAB <= 32 and TOK == E * SLOT
OUT_AFTER = 3
XIN = 4
YIN = 16


def columns(g):
    out = []
    for c in range(CPB):
        for kt in range(TPC * (c + 1)):
            out.append((c, kt, max(0, kt * PART - c * BANK), kt >= c * TPC))
    return out


NCOL = len(columns(0))


MID = GPB * NCOL
SCATTER0 = 10
XT0 = 29


def spread(start):
    out, m, n = {}, 0, start
    while m < TOPK * NT:
        k = 2 if start < MID else 1
        out[n] = list(range(m, min(m + k, TOPK * NT)))
        m += k
        n += 1
    return out


SCATTERS, GATHERS = spread(SCATTER0), spread(MID)
SCATTERED = max(SCATTERS) + 1


def max_work(item):
    if item[0] == "mT":
        return 0
    return (item[-1] + 1) * PART * (2 if item[0] == "max2" else 1) + 150


ACT_TAKES = ("turn", "aT", "cT")


def max_items(g, c):
    if c:
        return [("max1", g, j, i) for j in range(G4) for i in range(KT - 1, TPC - 1, -1)]
    return [("max2", g, j, i) for j in range(0, G4, 2) for i in range(TPC)]


LEAD = 1.01
RAMP = (0.7, 0.85, 1.0)
FIXED = 150
WIDTH = sum(BANK - col[2] + FIXED for col in columns(0)) / BANK
def schedule():
    stream, last = [], None
    for g in range(NG):
        for c in range(CPB):
            items = max_items(g, c)
            if last:
                items.insert(2, ("mT", *last))
            stream += items
            last = g, c
    stream.append(("mT", *last))
    ahead = stream.index(("mT", 0, 0)) + 1 + 5
    first, rest = stream[:ahead], stream[ahead:]
    slots = []
    given = turned = wide = 0
    taken = sum(max_work(item) for item in first)
    group = sum(max_work(item) for c in range(CPB) for item in max_items(0, c))
    for n in range(NG * NCOL):
        wide += (BANK - columns(0)[n % NCOL][2] + FIXED) / BANK
        want = group * (RAMP[n] if n < len(RAMP) else LEAD + wide / WIDTH)
        here = []
        while given < len(rest) and (taken < want or rest[given][0] == "mT"):
            here.append(rest[given])
            taken += max_work(rest[given])
            given += 1
        g, k = divmod(n, NCOL)
        if n == 6:
            here.append(("count",))
        if XT0 <= n < MID:
            want = SLOTS // 2 * (n + 1 - XT0) // (MID - XT0)
            here += [("turn", s) for s in range(turned, want)]
            turned = want
        if n == NG * NCOL - NCOL:
            here += [("cT", B - 1, 0)]
        if NG * NCOL - 5 <= n < NG * NCOL - 2:
            here += [[("aT", B - 1, 0)], [("wo", B - 1, 0)], [("cT", B - 1, 1)]][n - (NG * NCOL - 5)]
        if g % GPB == 0 and g and 2 <= k < 6:
            b, c = g // GPB - 1, (k - 2) // 2
            here += [("aT", b, c), ("cT", b, c)] if k % 2 == 0 else [("wo", b, c)]
        if k == TPC + 2:
            here.append(("oT", g, 0))
        if k == 2 and g:
            here.append(("oT", g - 1, 1))
        slots.append(here)
    tail = [("oT", NG - 1, 1)] + [("aT", B - 1, 1), ("wo", B - 1, 1)]
    return first, slots, tail


def parts(items):
    out = [[] for _ in range(G4)]
    for i, item in enumerate(items):
        out[(2 * i + 1) * G4 // (2 * len(items))].append(item)
    return out


def score_banks(slots):
    last = max(n for n in range(NG * NCOL) if any(item[0] in ("max1", "max2", "mT") for item in slots[n]))
    banks, wide = [], (4, 5, 6, 0, 1)
    for u in range(NG * NCOL * G4):
        banks.append(wide[u % 5] if u // G4 > last else 4 + u % 3)
    return last, banks


def build(nc, x, wpack, w12, w3, b3, rope, kappa, out):
    first, slots, tail = schedule()
    ring_order = first + [i for s in slots for i in s] + tail
    ring_at = {item: r for r, item in enumerate(ring_order)}
    last_max, sbank = score_banks(slots)
    wide_ring = len(first) + sum(len(s) for s in slots[:last_max + 1])

    by_act = [item[0] in ACT_TAKES for item in ring_order]

    def ring_bank(r):
        return 2 * (r % 2) if r < wide_ring else 2

    mid_ring = len(first) + sum(len(s) for s in slots[:MID])
    qkbuf = nc.dram_tensor("qkbuf", [B, NH, HD, 4 * T], F16).ap()
    maxbuf = nc.dram_tensor("maxbuf", [NG, CPB, 2, G4, BANK], F16).ap()
    xbuf = nc.dram_tensor("xbuf", [SLOTS * SLOT, 2 * D], F16).ap()
    ybuf = nc.dram_tensor("ybuf", [SLOTS * SLOT, D], F32).ap()

    with ExitStack() as ctx:
        def sb(name, shape, dt, scope=ctx):
            return scope.enter_context(nc.sbuf_tensor(name, shape, dt))

        def sem(name):
            return ctx.enter_context(nc.semaphore(name))

        acc = sb("acc", [PART, NT, D], F32)
        pack = sb("pack", [PART, PACK_COLS], F32)
        b3_sb = sb("b3_sb", [E, D], F32)
        identf = sb("identf", [PART, PART], F32)
        identh = sb("identh", [PART, PART], F16)
        identb = sb("identb", [PART, PART], BF16)
        causal = sb("causal", [PART, PART], BF16)
        before = sb("before", [PART, PART], F16)
        ones_h = sb("ones_h", [PART, PART], F16)
        zeros = sb("zeros", [PART, 2 * D], F16)
        v_aug = sb("v_aug", [PART, NT, NH, HD + 1], F32)
        rope_s = sb("rope_s", [PART, TOK], F16)
        stack_a = sb("stack_a", [PART, G4, 2, T], F16)
        w_hi = sb("w_hi", [D, 2, E * FF], F16)
        w_lo = sb("w_lo", [D, 2, E * FF], F16)
        w3_sb = sb("w3_sb", [PART, E * FJ * D], F32)
        xin = sb("xin", [PART, XIN, SH, 2 * D], F16)
        comb = sb("comb", [PART, NT, E], F32)
        comb_t = sb("comb_t", [E, BANK], F32)
        wmix = sb("wmix", [PART, TOPK, NT], F32)
        rows_i = sb("rows_i", [PART, TOPK * NT], U32)
        etab = sb("etab", [PART, TAB], I32)
        b1_t = sb("b1_t", [PART, FJ, TAB], F32)
        b2_t = sb("b2_t", [PART, FJ, TAB], F32)
        b1_e = sb("b1_e", [PART, 2, FJ], F32)
        attn = sb("attn", [PART, KT, D], F32)
        attn_t = sb("attn_t", [D, CPB, BANK], F32)
        o_sb = sb("o_sb", [PART, 2, BANK], F32)
        rden = sb("rden", [PART, 2, TPC, G4], F32)
        maxima = sb("maxima", [PART, 2, G4, KT], F32)
        max_s = sb("max_s", [PART, 2, CPB, 2, G4, TPC], F16)
        max_t = sb("max_t", [2 * G4 * TPC, CPB, PART], F16)
        amax = sb("amax", [PART, 8], F32)
        amax_all = sb("amax_all", [PART, 8], F32)
        pow2 = sb("pow2", [PART, 8], F32)
        ipow = sb("ipow", [PART, 8], F32)
        scales = sb("scales", [PART, 10], F32)
        ALPHA, BETA, TMP, A1, IA1, A2, IA2, TMP2 = (scales[:, i:i + 1] for i in range(8))
        b2_s = sb("b2_s", [PART, E * FJ], F32)
        logit = sb("logit", [PART, NT, E], F32)
        top = sb("top", [PART, NT, 8], F32)
        topi = sb("topi", [PART, NT, 8], U32)
        topf = sb("topf", [PART, NT, 8], F32)
        rw = sb("rw", [PART, 4, NT], F32)
        eq = sb("eq", [PART, TOPK, NT, E], F32)
        sel = sb("sel", [PART, NT, E], F16)
        pos = sb("pos", [PART, NT, E], F32)
        picked = sb("picked", [PART, TOPK, NT, E], F32)
        rows_f = sb("rows_f", [PART, TOPK, NT], F32)
        slot_e = sb("slot_e", [PART, 2, TAB, E], F32)
        slot_f = sb("slot_f", [PART, 2, TAB], F32)
        small = sb("small", [PART, 2, E, E], F32)
        per_e = sb("per_e", [PART, 6, E], F32)

        planes1 = sb("planes1", [PART, 4, T], F16)
        with ExitStack() as scope:
            planes = [sb("planes0", [PART, 4, T], F16, scope), planes1]
        with ExitStack() as scope:
            hid = sb("hid", [PART, 2, FJ, SLOT], F32, scope)
            silu = sb("silu", [PART, 2, FJ, SLOT], F32, scope)
        y_in = sb("y_in", [PART, YIN, D], F32)
        with ExitStack() as scope:
            raw12 = sb("raw12", [D, 2, E * FF], F32, scope)
            x_rows = sb("x_rows", [PART, NT, 2 * D], F16, scope)
        xs = sb("xs", [PART, SLOTS, 2 * SLOT], F16)
        ys = xs[:, :, :].bitcast(F32)
        with ExitStack() as scope:
            c_t = sb("c_t", [D, TOK], F32, scope)
            rope_m = sb("rope_m", [PART, 2, NT, 2 * DR], F32, scope)
            rope_sum = sb("rope_sum", [PART, 2, NT, DR], F32, scope)
            rope_hl = sb("rope_hl", [PART, NT, 4, DR], F16, scope)
            rope_c = sb("rope_c", [PART, KT, 2 * DR], F32, scope)
            stats = sb("stats", [PART, NT, 6], F32, scope)
            mv = sb("mv", [PART, NT, 2], F32, scope)
            ln = sb("ln", [PART, 6, NT], F32, scope)
            used = 4 * (TOK + 2 * NT * 2 * DR + 2 * NT * DR + NT * 2 * DR + KT * 2 * DR + 14 * NT)
            sb("gap", [PART, (NH - G4) * 2 * T // 2 - used // 4], F32, scope)
            xn = sb("xn", [PART, NT, D], F32, scope)
            x_t = sb("x_t", [D, TOK], F32, scope)
        stack_b = sb("stack_b", [PART, NH - G4, 2, T], F16)
        probs = sb("probs", [PART, 3, G4, BANK], F32)

        ps = ctx.enter_context(nc.psum_tensor("ps", [PART, 8 * BANK], F32))

        def bank(n, a=0, b=BANK, p0=0, p1=PART):
            return ps[p0:p1, n * BANK + a:n * BANK + b]

        def plane(which, c):
            return planes[c // CPB][:, which, c % CPB * BANK:(c % CPB + 1) * BANK]

        def w(name):
            return pack[:, PACK[name][0]:PACK[name][1]]

        def stack(slot, rows, part, a=0, b=T):
            if slot < G4:
                return stack_a[rows[0]:rows[1], slot, part, a:b]
            return stack_b[rows[0]:rows[1], slot - G4, part, a:b]

        def stacks(first_slot, rows, part):
            if first_slot < G4:
                return stack_a[rows[0]:rows[1], :, part, :]
            return stack_b[rows[0]:rows[1], first_slot - G4:first_slot, part, :]

        ld_x = [sem(f"ld_x{c}") for c in range(NC)]
        ld_pack, ld_w12, ld_w3, ld_b3, ld_rope = (sem(n) for n in ("ld_pack", "ld_w12", "ld_w3", "ld_b3", "ld_rope"))
        pool_const = sem("pool_const")
        amax_done = sem("amax_done")
        amax_red = sem("amax_red")
        dve_chain = sem("dve_chain")
        pool_chain = sem("pool_chain")
        scales_ready = sem("scales_ready")
        var_ready = sem("var_ready")
        sqrt_done = sem("sqrt_done")
        xn_ready = sem("xn_ready")
        xt_ready, xt_done, xrow_done, rows_split = (sem(n) for n in ("xt_ready", "xt_done", "xrow_done", "rows_split"))
        q_ready, qhi_done, qlo_done = (sem(n) for n in ("q_ready", "qhi_done", "qlo_done"))
        c_ready, ct_done = sem("c_ready"), sem("ct_done")
        r_ready, rmul_done, radd_done, rhi_done, rlo_done, rt_ready, rope_done = (
            sem(n) for n in ("r_ready", "rmul_done", "radd_done", "rhi_done", "rlo_done", "rt_ready", "rope_done"))
        k_ready, khi_done, klo_done = (sem(n) for n in ("k_ready", "khi_done", "klo_done"))
        v_ready, v_done = sem("v_ready"), sem("v_done")
        logit_done = sem("logit_done")
        gate_ready, gap_ready, gexp_done, comb_ready = (
            sem(n) for n in ("gate_ready", "gap_ready", "gexp_done", "comb_ready"))
        sel_ready = sem("sel_ready")
        rows_ready = sem("rows_ready")
        table_ready = sem("table_ready")
        zeros_ready = sem("zeros_ready")
        filled = sem("filled")
        scattered = sem("scattered")
        slot_in = [sem(f"slot_in{i}") for i in range(XIN)]
        wsc_done, whi_done, wlo_done = sem("wsc_done"), sem("whi_done"), sem("wlo_done")
        up_g, up_v = sem("up_g"), sem("up_v")
        b1_done = sem("b1_done")
        silu_done = sem("silu_done")
        hid_done = sem("hid_done")
        down_ready = sem("down_ready")
        y_done = sem("y_done")
        stored = sem("stored")
        gathered = [sem(f"gathered{i}") for i in range(YIN)]
        mixed = sem("mixed")
        acc_done = sem("acc_done")
        load = [sem(f"load{g}") for g in range(NG)]
        mrow = [[sem(f"mrow{g}_{c}") for c in range(CPB)] for g in range(NG)]
        load0b = sem("load0b")
        mstore = [[sem(f"mstore{g}_{c}") for c in range(CPB)] for g in range(NG)]
        qk_store = [sem(f"qk_store{b}") for b in range(B)]
        ring_ready = sem("ring_ready")
        ring_done, ring_act = sem("ring_done"), sem("ring_act")
        msplit_done = sem("msplit_done")
        s_ready, exp_done = sem("s_ready"), sem("exp_done")
        mask_done = sem("mask_done")
        pv_done = sem("pv_done")
        o_done = sem("o_done")
        out_sem = sem("out_sem")

        def taken(r):
            return (ring_act, sum(by_act[:r + 1])) if by_act[r] else (ring_done, r + 1 - sum(by_act[:r + 1]))

        def last_before(r, act):
            return max(i for i in range(r) if by_act[i] == act)

        block = ctx.enter_context(nc.Block())

        @block.sync
        def _(sp):
            xv = x.rearrange("(c t p) d -> c p t d", p=PART, t=TPC)
            for c in range(NC):
                sp.dma_start(acc[:, c * TPC:(c + 1) * TPC, :], xv[c]).then_inc(ld_x[c], 16)
            for i in range(2):
                sp.dma_start(raw12[:, i, :], w12[i]).then_inc(ld_w12, 16)
            sp.dma_start(w3_sb[:, :], w3).then_inc(ld_w3, 16)
            sp.wait_ge(zeros_ready, 1)
            sp.dma_start(xbuf.rearrange("(q p) d -> p q d", p=PART),
                         zeros[:, :].unsqueeze(1).broadcast_to([PART, SLOTS * SH, 2 * D])).then_inc(filled, 16)

            def load_group(g):
                b, slot0 = g // GPB, G4 * (g % GPB)

                for a, z, done in ((0, BANK, load[g]), (BANK, T, load0b)) if g == 0 else ((0, T, load[g]),):
                    if g == 0 and a == 0:
                        load_heads(g)
                        sp.wait_ge(rope_done, 1)
                    for rows, part, src in (((0, 2), 0, (0, 64)), ((2, 3), 0, (0, 32)), ((0, 1), 1, (64, 96)),
                                            ((1, 3), 1, (64, 128))):
                        n = src[1] - src[0]
                        sp.dma_start(stacks(slot0, (HROW + rows[0] * DR, HROW + rows[1] * DR), part)[:, :, a:z],
                                     rope_s[src[0]:src[1], b * T + a:b * T + z].unsqueeze(1)
                                     .broadcast_to([n, G4, z - a])).then_inc(done, 16)
                if g:
                    load_heads(g)

            def load_heads(g):
                b, slot0 = g // GPB, G4 * (g % GPB)
                if b == 0:
                    sp.dma_start(stacks(slot0, (QK_ROWS, ALL_ROWS), 1),
                                 kappa.unsqueeze(1).broadcast_to([2, G4, T])).then_inc(load[g], 16)
                heads = qkbuf[b, G4 * (g % GPB):G4 * (g % GPB + 1)].rearrange("j d t -> d j t")
                st = stack_a[:, :] if slot0 == 0 else stack_b[:, slot0 - G4:slot0]
                for r, which in ((0, QLO), (1, QHI)):
                    sp.dma_start(st[r * HD:(r + 1) * HD].rearrange("d j q t -> d j (q t)"),
                                 heads[:, :, which * T:(which + 2) * T]).then_inc(load[g], 16)
                for part, which in ((0, QHI), (1, KHI)):
                    sp.dma_start(st[2 * HD:3 * HD, :, part], heads[:, :, which * T:(which + 1) * T]
                                 ).then_inc(load[g], 16)

            def store_maxima(g, c):
                sp.wait_ge(*taken(ring_at["mT", g, c]))
                sp.dma_start(maxbuf[g, c].rearrange("s j (i t) -> (s j i) t", t=PART), max_t[:, c, :]
                             ).then_inc(mstore[g][c], 16)
                sp.wait_ge(mstore[g][c], 16)
                slot0 = G4 * (g % GPB)
                st = stack_a[:, :] if slot0 == 0 else stack_b[:, slot0 - G4:slot0]
                sp.dma_start(st[QK_ROWS:ALL_ROWS, :, 0, c * BANK:(c + 1) * BANK], maxbuf[g, c]
                             ).then_inc(mrow[g][c], 16)

            def load_slot(s):
                sp.dma_start(xin[:, s % XIN], xbuf[s * SLOT:(s + 1) * SLOT, :].rearrange("(h p) d -> p h d", p=PART)
                             ).then_inc(slot_in[s % XIN], 16)

            ov = out.rearrange("(c t p) d -> c p t d", p=PART, t=TPC)

            def store_out(b):
                for c in range(CPB):
                    n = b * CPB + c
                    sp.wait_ge(*taken(ring_at["wo", b, c]))
                    sp.wait_ge(mixed, TOPK * TPC * (n + 1))
                    sp.dma_start(ov[n], acc[:, n * TPC:(n + 1) * TPC, :]).then_inc(out_sem, 16)

            for b in range(B):
                for s in (qhi_done, qlo_done, khi_done, klo_done):
                    sp.wait_ge(s, CPB * (b + 1))
                sp.dma_start(qkbuf[b].rearrange("h d t -> (h d) t"), planes[b].rearrange("p k t -> p (k t)")
                             ).then_inc(qk_store[b], 16)
            sp.wait_ge(qk_store[0], 16)
            load_group(0)
            sp.wait_ge(v_ready, NC)
            sp.wait_ge(rope_done, B)
            sp.wait_ge(xn_ready, NT)
            store_maxima(0, 0)
            load_group(1)
            for n in range(NG * NCOL):
                if n == SCATTERED:
                    sp.wait_ge(scattered, 16 * TOPK * NT)
                    for s in range(XIN):
                        load_slot(s)
                if n == MID:
                    for s in range(0, SLOTS, 4):
                        sp.wait_ge(y_done, 2 + s + 4)
                        sp.dma_start(ybuf[s * SLOT:(s + 4) * SLOT, :].rearrange("(h p) d -> p h d", p=PART),
                                     ys[:, s:s + 4].rearrange("p s (h d) -> p (s h) d", d=D)).then_inc(stored, 16)
                if n == NG * NCOL - NCOL:
                    store_out(0)
                for item in slots[n]:
                    if item[0] == "mT":
                        store_maxima(*item[1:])
                        g = item[1] + 2
                        if item[2] == 1 and g < NG:
                            if g >= GPB:
                                sp.wait_ge(qk_store[1], 16)
                                sp.wait_ge(s_ready, G4 * NCOL * (g - GPB + 1))
                            load_group(g)
                    if item[0] == "turn" and 2 * item[1] + XIN < SLOTS:
                        sp.wait_ge(ring_ready, ring_at[item] + 1)
                        for k in range(2):
                            load_slot(2 * item[1] + k + XIN)
            for b in range(1, B):
                store_out(b)
            sp.wait_ge(out_sem, 16 * NC)
            sp.wait_ge(filled, 16)
            sp.wait_ge(scattered, 16 * TOPK * NT)
            sp.wait_ge(stored, 16 * (SLOTS // 4))

        @block.gpsimd
        def _(pool):
            pool.memset(identf[:, :], 0.0).then_inc(pool_chain, 1)
            pool.memset(causal[:, :], 0.0).then_inc(pool_chain, 1)
            pool.wait_ge(pool_chain, 1)
            pool.affine_select(out=identf[:, :], in_=identf[:, :], compare_op=ALU.not_equal, fill=1.0, base=0,
                               pattern=[[-1, PART]], channel_multiplier=1).then_inc(pool_const, 1)
            pool.wait_ge(pool_const, 1)
            pool.tensor_copy(identh[:, :], identf[:, :]).then_inc(pool_const, 1)
            pool.tensor_copy(identb[:, :], identf[:, :]).then_inc(pool_const, 1)
            pool.memset(zeros[:, :], 0.0).then_inc(zeros_ready, 1)
            pool.wait_ge(amax_done, 3)
            pool.partition_all_reduce(amax_all[:, 0:3], amax[:, 0:3], PART, bass.bass_isa.ReduceOp.max
                                      ).then_inc(amax_red, 1)
            pool.wait_ge(pool_chain, 2)
            pool.affine_select(out=causal[:, :], in_=causal[:, :], compare_op=ALU.is_ge, fill=NEG, base=0,
                               pattern=[[-1, PART]], channel_multiplier=1).then_inc(pool_const, 1)
            pool.memset(v_aug[:, :, :, HD:HD + 1], 1.0).then_inc(pool_const, 1)
            pool.memset(ones_h[:, :], 1.0).then_inc(pool_chain, 1)
            pool.wait_ge(pool_chain, 3)
            pool.affine_select(out=before[:, :], in_=ones_h[:, :], compare_op=ALU.is_ge, fill=0.0, base=-1,
                               pattern=[[1, PART]], channel_multiplier=-1).then_inc(pool_const, 1)
            pool.wait_ge(amax_done, 5)
            pool.partition_all_reduce(amax_all[:, 3:5], amax[:, 3:5], PART, bass.bass_isa.ReduceOp.max
                                      ).then_inc(amax_red, 1)

            pool.wait_ge(xn_ready, NT)
            pool.wait_ge(xrow_done, 1)
            pool.tensor_tensor(x_rows[:, :, D:2 * D], xn[:, :, :], x_rows[:, :, 0:D], ALU.subtract
                               ).then_inc(rows_split, 1)

            def split_weights(i, half):
                cols = slice(half * E * FF // 2, (half + 1) * E * FF // 2)
                pool.wait_ge(whi_done, i + 1)
                pool.tensor_tensor(w_lo[:, i, cols], raw12[:, i, cols], w_hi[:, i, cols], ALU.subtract
                                   ).then_inc(wlo_done, 1)

            for i in range(2):
                for half in range(2):
                    split_weights(i, half)

            def scatter(m):
                k, t = m % TOPK, m // TOPK
                if m == 0:
                    pool.wait_ge(filled, 16)
                    pool.wait_ge(rows_ready, 1)
                    pool.wait_ge(rows_split, 1)
                pool.indirect_dma_start(xbuf, bass.IndirectOffsetOnAxis(rows_i[:, k * NT + t:k * NT + t + 1], 0),
                                        x_rows[:, t, :], None, bounds_check=SLOTS * SLOT - 1, oob_is_err=False
                                        ).then_inc(scattered, 16)

            def gather(m):
                k, t = m % TOPK, m // TOPK
                if m == 0:
                    pool.wait_ge(stored, 16 * (SLOTS // 4))
                if m >= YIN:
                    pool.wait_ge(mixed, m - YIN + 1)
                pool.indirect_dma_start(y_in[:, m % YIN, :], None, ybuf,
                                        bass.IndirectOffsetOnAxis(rows_i[:, k * NT + t:k * NT + t + 1], 0),
                                        bounds_check=SLOTS * SLOT - 1, oob_is_err=False
                                        ).then_inc(gathered[m % YIN], 16)

            for n in range(NG * NCOL):
                c, kt, at, diagonal = columns(0)[n % NCOL]
                if diagonal:
                    pool.wait_ge(exp_done, G4 * (n + 1))
                    p = probs[:, n % 3, :, at:at + PART]
                    pool.affine_select(out=p, in_=p, compare_op=ALU.is_ge, fill=0.0, base=0,
                                       pattern=[[0, G4], [1, PART]], channel_multiplier=-1
                                       ).then_inc(mask_done, 1)
                for m in SCATTERS.get(n, ()):
                    scatter(m)
                for m in GATHERS.get(n, ()):
                    gather(m)

        @block.scalar
        def _(act):
            act.dma_start(pack[:, :], wpack).then_inc(ld_pack, 16)
            act.dma_start(rope_c[:, :, :], rope).then_inc(ld_rope, 16)
            act.dma_start(b3_sb[:, :], b3).then_inc(ld_b3, 16)
            for b in range(B):
                tiles = slice(b * KT, (b + 1) * KT)
                act.wait_ge(var_ready, b + 1)
                act.activation(ln[:, 1, tiles], ln[:, 0, tiles], ACT.Sqrt).then_inc(sqrt_done, 1)
                for c in range(b * CPB, (b + 1) * CPB):
                    act.wait_ge(xt_ready, c + 1)
                    act.activation(x_t[:, c * BANK:(c + 1) * BANK], bank(c), ACT.Copy).then_inc(xt_done, 1)
                for c in range(b * CPB, (b + 1) * CPB):
                    act.wait_ge(c_ready, c + 1)
                    act.activation(c_t[:, c * BANK:(c + 1) * BANK], bank(c), ACT.Copy).then_inc(ct_done, 1)
            act.wait_ge(scales_ready, 1)
            for c in range(NC):
                act.wait_ge(q_ready, c + 1)
                act.activation(plane(QHI, c), bank(4 + c), ACT.Copy, scale=ALPHA).then_inc(qhi_done, 1)
            for c in range(NC):
                act.wait_ge(k_ready, c + 1)
                act.activation(plane(KHI, c), bank(c), ACT.Copy, scale=BETA).then_inc(khi_done, 1)

            def rope_high(b, s):
                tiles = slice(b * KT, (b + 1) * KT)
                act.wait_ge(radd_done, 2 * b + s + 1)
                act.activation(rope_hl[:, tiles, 2 * s, :], rope_sum[:, s, tiles], ACT.Copy, scale=scales[:, s:s + 1]
                               ).then_inc(rhi_done, 1)

            def rope_back(b):
                act.wait_ge(rt_ready, b + 1)
                act.activation(rope_s[:, b * T:(b + 1) * T], bank(4 + 2 * b).bitcast(F16), ACT.Copy
                               ).then_inc(rope_done, 1)

            rope_high(0, 0)
            rope_high(0, 1)
            rope_high(1, 0)
            rope_back(0)
            rope_high(1, 1)
            rope_back(1)
            act.activation(x_rows[:, :, 0:D], xn[:, :, :], ACT.Copy).then_inc(xrow_done, 1)
            for c in range(NC):
                act.wait_ge(v_ready, c + 1)
                act.activation(v_aug[:, c * TPC:(c + 1) * TPC, :, 0:HD],
                               bank(c).rearrange("p (t h d) -> p t h d", t=TPC, h=NH), ACT.Copy).then_inc(v_done, 1)

            def gates(s, k):
                act.wait_ge(up_g, s + 1)
                act.wait_ge(b1_done, s + 1)
                for j in range(FJ):
                    ins = act.activation(silu[:, k, j, :], bank(k, j * SLOT, (j + 1) * SLOT), ACT.Silu,
                                         bias=b1_e[:, k, j:j + 1], scale=IA1)
                ins.then_inc(silu_done, 1)

            def ring_results(items):
                for item in items:
                    r, b0 = ring_at[item], ring_bank(ring_at[item])
                    if not by_act[r]:
                        continue
                    act.wait_ge(ring_ready, r + 1)
                    if item[0] == "turn":
                        act.wait_ge(wlo_done, 4)
                        act.wait_ge(scattered, 16 * TOPK * NT)
                        two = xs[:, 2 * item[1]:2 * item[1] + 2, :].rearrange("p s n -> p (s n)")
                        ins = act.activation(two, bank(b0).bitcast(F16), ACT.Copy)
                    elif item[0] == "aT":
                        ins = act.activation(attn_t[:, item[2], :], bank(b0), ACT.Copy)
                    else:
                        ins = act.activation(comb_t[:, :], bank(b0, p1=E), ACT.Copy)
                    ins.then_inc(ring_act, 1)

            def output_rows(q):
                act.wait_ge(pv_done, NCOL * (q // CPB) + (TPC, NCOL)[q % CPB])
                if q >= 2:
                    act.wait_ge(ring_ready, ring_at["oT", (q - 2) // CPB, q % CPB] + 1)
                act.activation(o_sb[:, q % 2, :], bank(7), ACT.Copy).then_inc(o_done, 1)

            act.wait_ge(scales_ready, 2)
            for i, a in enumerate((A1, A2)):
                act.activation(w_hi[:, i, :], raw12[:, i, :], ACT.Copy, scale=a).then_inc(wsc_done, 1)
                act.wait_ge(wsc_done, i + 1)
                act.activation(raw12[:, i, :], raw12[:, i, :], ACT.Copy, scale=a).then_inc(whi_done, 1)
            act.wait_ge(rows_split, 1)
            act.wait_ge(gate_ready, 1)
            u = 0
            for g in range(NG):
                if g * NCOL == MID:
                    for k in range(2):
                        gates(k, k)
                    with act.Fori(1, SLOTS // 2) as i:
                        for k in range(2):
                            gates(2 * i + k, k)
                for k, (c, kt, at, _) in enumerate(columns(g)):
                    n = g * NCOL + k
                    if n == 8:
                        act.wait_ge(gap_ready, 1)
                        act.activation(rw[:, 1, :], rw[:, 0, :], ACT.Exp).then_inc(gexp_done, 1)
                    for j in range(G4):
                        act.wait_ge(s_ready, u + 1)
                        if n >= 3 and j == 0:
                            act.wait_ge(pv_done, n - 2)
                        act.activation(probs[:, n % 3, j, at:BANK], bank(sbank[u], at), ACT.Exp, scale=float(EXP_SCALE)
                                       ).then_inc(exp_done, 1)
                        u += 1
                        ring = parts(slots[n])
                        if j:
                            ring_results(ring[j - 1])
                        if j == G4 - 1:
                            ring_results(ring[j])
                        if j == OUT_AFTER and k == TPC + 1:
                            output_rows(CPB * g)
                        if j == OUT_AFTER and k == 1 and g:
                            output_rows(CPB * g - 1)
            output_rows(CPB * NG - 1)
            ring_results(tail)

        @block.tensor
        def _(pe):
            pe.wait_ge(pool_const, 3)
            for b in range(B):
                for t in range(b * KT, (b + 1) * KT):
                    pe.wait_ge(xn_ready, t + 1)
                    mm = pe.transpose(bank(t // TPC, t % TPC * PART, t % TPC * PART + PART), xn[:, t, :],
                                      identf[:, :])
                    if t % TPC == TPC - 1:
                        mm.then_inc(xt_ready, 1)
                pe.wait_ge(ld_pack, 16)
                for c in range(b * CPB, (b + 1) * CPB):
                    pe.wait_ge(xt_done, c + 1)
                    pe.matmul(bank(c), w("wkv"), x_t[:, c * BANK:(c + 1) * BANK], start=True, stop=True
                              ).then_inc(c_ready, 1)
                for c in range(b * CPB, (b + 1) * CPB):
                    pe.matmul(bank(4 + c), w("wq"), x_t[:, c * BANK:(c + 1) * BANK], start=True, stop=True
                              ).then_inc(q_ready, 1)
            for c in range(NC):
                pe.wait_ge(ct_done, c + 1)
                pe.matmul(bank(c), w("wk"), c_t[:, c * BANK:(c + 1) * BANK], start=True, stop=True
                          ).then_inc(k_ready, 1)

            def rotary(b, s):
                n = 2 * b + s
                pe.wait_ge(qhi_done, n + 1)
                pe.wait_ge(qlo_done, n + 1)
                source, weights = ((x_t, w("wqr")), (c_t, w("wkr")))[s]
                for t in range(KT):
                    at = (b * KT + t) * PART
                    mm = pe.matmul(bank(4 + n, t * 2 * DR, (t + 1) * 2 * DR), source[:, at:at + PART], weights,
                                   start=True, stop=True)
                mm.then_inc(r_ready, 1)

            def rotary_back(b):
                pe.wait_ge(rhi_done, 2 * b + 2)
                pe.wait_ge(rlo_done, 2 * b + 2)
                for t in range(KT):
                    mm = pe.transpose(bank(4 + 2 * b, t * PART // 2, (t + 1) * PART // 2).bitcast(F16),
                                      rope_hl[:, b * KT + t].rearrange("p k d -> p (k d)"), identh[:, :])
                mm.then_inc(rt_ready, 1)

            def values(c):
                pe.wait_ge(khi_done, c + 1)
                pe.wait_ge(klo_done, c + 1)
                for t in range(TPC):
                    at = (c * TPC + t) * PART
                    mm = pe.matmul(bank(c, t * PART, (t + 1) * PART), c_t[:, at:at + PART], w("wv"),
                                   start=True, stop=True)
                mm.then_inc(v_ready, 1)

            for b in range(B):
                for s in range(2):
                    rotary(b, s)
            rotary_back(0)
            values(0)
            values(1)
            rotary_back(1)
            values(2)
            values(3)
            for t in range(NT):
                mm = pe.matmul(bank(5, t * E, (t + 1) * E), x_t[:, t * PART:(t + 1) * PART], w("wg"),
                               start=True, stop=True)
            mm.then_inc(gate_ready, 1)
            pe.wait_ge(v_done, NC)
            pe.wait_ge(rope_done, B)
            pe.wait_ge(pool_const, 6)
            pe.wait_ge(logit_done, 1)

            def up(s, k, e):
                for i, ready in enumerate((up_g, up_v)):
                    for j in range(FJ):
                        dst = bank(2 * i + k, j * SLOT, (j + 1) * SLOT)
                        hi = w_hi[:, i, bass.ds(e + j * PART, PART)]
                        lo = w_lo[:, i, bass.ds(e + j * PART, PART)]
                        x_hi, x_lo = (xs[:, s, a * SLOT:(a + 1) * SLOT] for a in range(2))
                        pe.matmul(dst, hi, x_hi, start=True, stop=False)
                        pe.matmul(dst, hi, x_lo, start=False, stop=False)
                        mm = pe.matmul(dst, lo, x_hi, start=False, stop=True)
                    mm.then_inc(ready, 1)

            def down(k, e):
                parts = [w3_sb[:, bass.ds(e + j * D, D)] for j in range(FJ)]
                for h in range(SH):
                    for j in range(FJ):
                        mm = pe.matmul(bank(4 + k, h * D, (h + 1) * D), hid[:, k, j, h * PART:(h + 1) * PART],
                                       parts[j], start=(j == 0), stop=(j == FJ - 1))
                mm.then_inc(down_ready, 1)

            def experts_of(s, n):
                _, values = nc.values_load_multi_w_load_instructions(
                    etab[0:1, bass.ds(s, n)], engines=[mybir.EngineType.PE], min_val=0, max_val=(E - 1) * FF,
                    skip_runtime_bounds_check_because="DVE has clamped the expert to E - 1")
                return values

            def experts():
                pe.sem_inc(down_ready, 2)
                for act in (False, True):
                    pe.wait_ge(*taken(last_before(mid_ring, act)))
                pe.wait_ge(exp_done, G4 * MID)
                pe.wait_ge(ld_w3, 16)
                pe.wait_ge(wlo_done, 4)
                pe.wait_ge(table_ready, 1)
                es = experts_of(0, 2)
                for s in range(2):
                    up(s, s, es[s])
                with pe.Fori(1, SLOTS // 2) as i:
                    es = experts_of(2 * i - 2, 4)
                    for k in range(2):
                        s = 2 * i + k
                        pe.wait_ge(hid_done, s - 1)
                        up(s, k, es[2 + k])
                        pe.wait_ge(y_done, s - 1)
                        down(k, es[k])
                es = experts_of(SLOTS - 2, 2)
                for k in range(2):
                    pe.wait_ge(hid_done, SLOTS - 1 + k)
                    pe.wait_ge(y_done, SLOTS - 1 + k)
                    down(k, es[k])
                pe.wait_ge(y_done, 2 + SLOTS)

            def ring_job(item):
                r = ring_at[item]
                kind = item[0]
                b0 = ring_bank(r)
                if r >= 2:
                    pe.wait_ge(*taken(r - 2 if r < wide_ring else r - 1))
                if kind == "max1":
                    _, g, j, i = item
                    slot = G4 * (g % GPB) + j
                    q = stack(slot, (0, QK_ROWS), 0, i * PART, (i + 1) * PART)
                    end = (i + 1) * PART
                    pe.matmul(bank(b0), q, stack(slot, (0, QK_ROWS), 1, 0, BANK), start=True, stop=True)
                    pe.matmul(bank(b0 + 1, 0, end - BANK), q, stack(slot, (0, QK_ROWS), 1, BANK, end),
                              start=True, stop=False)
                    mm = pe.matmul(bank(b0 + 1, end - BANK - PART, end - BANK), identb[:, :], causal[:, :],
                                   start=False, stop=True)
                elif kind == "max2":
                    _, g, j, i = item
                    end = (i + 1) * PART
                    for k in range(2):
                        slot = G4 * (g % GPB) + j + k
                        pe.matmul(bank(b0 + k, 0, end), stack(slot, (0, QK_ROWS), 0, i * PART, end),
                                  stack(slot, (0, QK_ROWS), 1, 0, end), start=True, stop=False)
                        mm = pe.matmul(bank(b0 + k, end - PART, end), identb[:, :], causal[:, :],
                                       start=False, stop=True)
                elif kind == "mT":
                    g = item[1]
                    pe.wait_ge(msplit_done, 2 * (CPB * g + item[2] + 1))
                    mm = pe.transpose(bank(b0, 0, PART // 2, p1=2 * G4 * TPC).bitcast(F16),
                                      max_s[:, g % 2, item[2]].rearrange("p s j i -> p (s j i)"), identh[:, :])
                elif kind == "oT":
                    q = item[1] * CPB + item[2]
                    pe.wait_ge(o_done, q + 1)
                    for t in range(TPC):
                        mm = pe.transpose(bank(b0, t * PART, (t + 1) * PART),
                                          o_sb[:, q % 2, t * PART:(t + 1) * PART], identf[:, :])
                elif kind == "aT":
                    _, b, c = item
                    pe.wait_ge(*taken(ring_at["oT", GPB * (b + 1) - 1, c]))
                    for t in range(TPC):
                        mm = pe.transpose(bank(b0, t * PART, (t + 1) * PART), attn[:, c * TPC + t, :],
                                          identf[:, :])
                elif kind == "cT":
                    _, b, c = item
                    pe.wait_ge(comb_ready, 1)
                    for t in range(TPC):
                        mm = pe.transpose(bank(b0, t * PART, (t + 1) * PART, p1=E),
                                          comb[:, b * KT + c * TPC + t, :], identf[:, :])
                elif kind == "count":
                    pe.wait_ge(sel_ready, 1)
                    pe.wait_ge(pool_const, 6)
                    mm = pe.matmul(bank(b0, 0, NT * E), before[:, :], sel.rearrange("p t e -> p (t e)"),
                                   start=True, stop=False)
                    for t in range(NT - 1):
                        pe.matmul(bank(b0, (t + 1) * E, NT * E), ones_h[:, :],
                                  sel[:, t:t + 1, :].broadcast_to([PART, NT - 1 - t, E]),
                                  start=False, stop=(t == NT - 2))
                    for t in range(NT):
                        mm = pe.matmul(bank(b0 + 1, 0, E), ones_h[:, :], sel[:, t, :], start=(t == 0),
                                       stop=(t == NT - 1))
                elif kind == "turn":
                    for k in range(2):
                        s = 2 * item[1] + k
                        pe.wait_ge(slot_in[s % XIN], 16 * (s // XIN + 1))
                        for h in range(SH):
                            for a in range(2):
                                at = k * SLOT + (a * SLOT + h * PART) // 2
                                mm = pe.transpose(bank(b0, at, at + PART // 2).bitcast(F16),
                                                  xin[:, s % XIN, h, a * D:(a + 1) * D], identh[:, :])
                else:
                    _, b, c = item
                    pe.wait_ge(*taken(ring_at["aT", b, c]))
                    pe.wait_ge(*taken(ring_at["cT", b, c]))
                    for t in range(TPC):
                        tile = b * KT + c * TPC + t
                        pe.matmul(bank(b0, t * PART, (t + 1) * PART), attn_t[:, c, t * PART:(t + 1) * PART],
                                  w("wo"), start=True, stop=False)
                        mm = pe.matmul(bank(b0, t * PART, (t + 1) * PART),
                                       comb_t[:, t * PART:(t + 1) * PART], b3_sb[:, :],
                                       start=False, stop=True)
                mm.then_inc(ring_ready, 1)

            def prob_values(n, half):
                g, k = divmod(n, NCOL)
                c, kt, at, diagonal = columns(g)[k]
                q = CPB * g + c
                tile = KT * (g // GPB) + kt
                tiles = (BANK - at) // PART
                middle = at if kt == 0 else at + (tiles + 1) // 2 * PART
                a, z = ((at, middle), (middle, BANK))[half]
                if a == z:
                    return
                pe.wait_ge(exp_done, G4 * (n + 1))
                if diagonal:
                    pe.wait_ge(mask_done, masks[n])
                if kt == 0 and q >= 1:
                    pe.wait_ge(o_done, q)
                for j in range(G4):
                    mm = pe.matmul(bank(7, a, z, p0=32 * j, p1=32 * j + HD + 1),
                                   v_aug[:, tile, G4 * (g % GPB) + j, :], probs[:, n % 3, j, a:z],
                                   start=(kt == 0), stop=(kt == TPC * (c + 1) - 1))
                if z == BANK:
                    mm.then_inc(pv_done, 1)

            masks, found = {}, 0
            for n in range(NG * NCOL):
                if columns(0)[n % NCOL][3]:
                    found += 1
                    masks[n] = found

            pe.wait_ge(ld_b3, 16)
            loads = {}

            def stacks_loaded(g):
                if g not in loads:
                    loads[g] = True
                    pe.wait_ge(load[g], 16 * (4 + (g < GPB) + 4))

            def run_ring(items):
                for item in items:
                    if item[0] in ("max1", "max2"):
                        stacks_loaded(item[1])
                    if item[0] == "max1" and "0b" not in loads:
                        loads["0b"] = True
                        pe.wait_ge(load0b, 16 * 4)
                    ring_job(item)

            run_ring(first)
            u = 0
            for g in range(NG):
                if g * NCOL == MID:
                    for m in (MID - 2, MID - 1):
                        for i in range(2):
                            prob_values(m, i)
                    experts()
                for k, (c, kt, at, _) in enumerate(columns(g)):
                    n = g * NCOL + k
                    ring = parts(slots[n])
                    if kt == 0:
                        pe.wait_ge(mrow[g][c], 16)
                    for j in range(G4):
                        slot = G4 * (g % GPB) + j
                        before_u = [v for v in range(u) if sbank[v] == sbank[u]]
                        if before_u:
                            pe.wait_ge(exp_done, before_u[-1] + 1)
                        if sbank[u] < 4 and len(before_u) == 0:
                            for act in (False, True):
                                pe.wait_ge(*taken(last_before(wide_ring, act)))
                        pe.matmul(bank(sbank[u], at), stack(slot, (0, ALL_ROWS), 1, kt * PART, (kt + 1) * PART),
                                  stack(slot, (0, ALL_ROWS), 0, c * BANK + at, (c + 1) * BANK),
                                  start=True, stop=True).then_inc(s_ready, 1)
                        u += 1
                        if j % 2 == 0 and n >= 2 and n not in (MID, MID + 1):
                            prob_values(n - 2, j // 2)
                        run_ring(ring[j])
            for m in (NG * NCOL - 2, NG * NCOL - 1):
                for i in range(2):
                    prob_values(m, i)
            run_ring(tail)

        @block.vector
        def _(dve):
            chained = [0]

            def step(ins):
                chained[0] += 1
                return ins.then_inc(dve_chain, 1)

            def settle():
                dve.wait_ge(dve_chain, chained[0])

            for b in range(B):
                tiles = slice(b * KT, (b + 1) * KT)
                for c in range(b * CPB, (b + 1) * CPB):
                    dve.wait_ge(ld_x[c], 16)
                    for t in range(c * TPC, (c + 1) * TPC):
                        step(dve.bn_stats(stats[:, t, :], acc[:, t, :]))
                settle()
                for t in range(b * KT, (b + 1) * KT):
                    step(dve.bn_aggr(mv[:, t, :], stats[:, t, :]))
                settle()
                dve.tensor_scalar(ln[:, 0, tiles], mv[:, tiles, 1], EPS, None, ALU.add).then_inc(var_ready, 1)
                dve.wait_ge(sqrt_done, b + 1)
                step(dve.reciprocal(ln[:, 2, tiles], ln[:, 1, tiles]))
                settle()
                step(dve.tensor_tensor(ln[:, 3, tiles], ln[:, 0, tiles], ln[:, 2, tiles], ALU.mult))
                settle()
                step(dve.tensor_tensor(ln[:, 4, tiles], ln[:, 3, tiles], ln[:, 1, tiles], ALU.add))
                settle()
                step(dve.tensor_scalar(ln[:, 2, tiles], ln[:, 4, tiles], 0.5, None, ALU.mult))
                settle()
                step(dve.reciprocal(ln[:, 5, tiles], ln[:, 2, tiles]))
                settle()
                for t in range(b * KT, (b + 1) * KT):
                    dve.tensor_scalar(xn[:, t, :], acc[:, t, :], mv[:, t, 0:1], ln[:, 5, t:t + 1],
                                      ALU.subtract, ALU.mult).then_inc(xn_ready, 1)
            dve.wait_ge(ld_pack, 16)
            for n, (a, b) in enumerate((("wq", "wqr"), ("wkv", "wkv"), ("wk", "wkr"))):
                dve.tensor_reduce(amax[:, n:n + 1], pack[:, PACK[a][0]:PACK[b][1]], AX.X, ALU.max,
                                  apply_absolute_value=True).then_inc(amax_done, 1)
            def powers(a, b):
                step(dve.tensor_scalar(pow2[:, a:b], amax_all[:, a:b], 2.0 ** -30, None, ALU.max))
                settle()
                step(dve.tensor_scalar(pow2[:, a:b].bitcast(I32), pow2[:, a:b].bitcast(I32), 0x7F800000, None,
                                       ALU.bitwise_and))
                settle()
                step(dve.reciprocal(ipow[:, a:b], pow2[:, a:b]))
                settle()
            dve.wait_ge(amax_red, 1)
            powers(0, 3)
            step(dve.tensor_scalar(TMP, pow2[:, 0:1], pow2[:, 1:2], pow2[:, 2:3], ALU.mult, ALU.mult))
            settle()
            step(dve.tensor_scalar(TMP.bitcast(I32), TMP.bitcast(I32), 1, 0x7F800000,
                                   ALU.logical_shift_right, ALU.bitwise_and))
            settle()
            step(dve.tensor_scalar(TMP, TMP, 2.0 ** 64, None, ALU.mult))
            settle()
            step(dve.tensor_scalar(ALPHA, ipow[:, 0:1], TMP, 2.0 ** 4, ALU.mult, ALU.mult))
            settle()
            step(dve.tensor_scalar(TMP2, ALPHA, 1.0 / QK_SCALE, None, ALU.mult))
            settle()
            step(dve.reciprocal(BETA, TMP2))
            settle()
            dve.sem_inc(scales_ready, 1)

            def low(plane_lo, plane_hi, b0, scale, hi_done, done):
                for c in range(NC):
                    dve.wait_ge(hi_done, c + 1)
                    dve.scalar_tensor_tensor(out=plane(plane_lo, c), in0=bank(b0 + c), scalar=scale,
                                             in1=plane(plane_hi, c), op0=ALU.mult, op1=ALU.subtract
                                             ).then_inc(done, 1)

            def rotate(b, s):
                n, tiles = 2 * b + s, slice(b * KT, (b + 1) * KT)
                dve.wait_ge(r_ready, n + 1)
                dve.tensor_tensor(rope_m[:, s, tiles], bank(4 + n).rearrange("p (t d) -> p t d", d=2 * DR),
                                  rope_c[:, :, :], ALU.mult).then_inc(rmul_done, 1)
                dve.wait_ge(rmul_done, n + 1)
                dve.tensor_tensor(rope_sum[:, s, tiles], rope_m[:, s, tiles, 0:DR], rope_m[:, s, tiles, DR:2 * DR],
                                  ALU.add).then_inc(radd_done, 1)

            def rope_low(b, s):
                tiles = slice(b * KT, (b + 1) * KT)
                dve.wait_ge(rhi_done, 2 * b + s + 1)
                dve.scalar_tensor_tensor(out=rope_hl[:, tiles, 2 * s + 1, :], in0=rope_sum[:, s, tiles],
                                         scalar=scales[:, s:s + 1], in1=rope_hl[:, tiles, 2 * s, :],
                                         op0=ALU.mult, op1=ALU.subtract).then_inc(rlo_done, 1)


            low(QLO, QHI, 4, ALPHA, qhi_done, qlo_done)
            low(KLO, KHI, 0, BETA, khi_done, klo_done)
            dve.wait_ge(ld_rope, 16)
            for b in range(B):
                for s in range(2):
                    rotate(b, s)
                for s in range(2):
                    rope_low(b, s)
            dve.wait_ge(ld_w12, 32)
            for i in range(2):
                dve.tensor_reduce(amax[:, 3 + i:4 + i], raw12[:, i, :], AX.X, ALU.max,
                                  apply_absolute_value=True).then_inc(amax_done, 1)
            dve.wait_ge(gate_ready, 1)
            dve.tensor_copy(logit[:, :, :], bank(5, 0, NT * E).rearrange("p (t e) -> p t e", e=E)
                            ).then_inc(logit_done, 1)

            iota = w("iota")

            def along(a, n):
                return a.unsqueeze(1).broadcast_to([PART, n, a.shape[1]])

            def across(a, n):
                return a.unsqueeze(2).broadcast_to([PART, a.shape[1], n])

            def route_choices():
                dve.wait_ge(logit_done, 1)
                for t in range(NT):
                    step(dve.max(top[:, t, :], logit[:, t, :]))
                settle()
                dve.tensor_tensor(rw[:, 0, :], top[:, :, 1], top[:, :, 0], ALU.subtract).then_inc(gap_ready, 1)
                for t in range(NT):
                    step(dve.max_index(topi[:, t, :], top[:, t, :], logit[:, t, :]))
                settle()
                step(dve.tensor_copy(topf[:, :, :], topi[:, :, :]))
                settle()
                for n in range(TOPK):
                    step(dve.tensor_tensor(eq[:, n], across(topf[:, :, n], E), along(iota[:, 0:E], NT), ALU.is_equal))
                settle()
                dve.tensor_tensor(sel[:, :, :], eq[:, 0], eq[:, 1], ALU.add).then_inc(sel_ready, 1)

            def route_rows():
                total, slots_of, end, start, limit = (per_e[:, i] for i in range(5))
                step(dve.tensor_scalar(limit, iota[:, 0:E], float(SLOT), None, ALU.mult))
                step(dve.tensor_tensor(small[:, 1], along(iota[:, 0:E], E), across(iota[:, 0:E], E), ALU.is_le))
                settle()
                step(dve.tensor_tensor(small[:, 0], across(total, E), along(limit, E), ALU.is_gt))
                settle()
                step(dve.tensor_reduce(slots_of, small[:, 0], AX.X, ALU.add))
                settle()
                step(dve.tensor_tensor(small[:, 0], small[:, 1], along(slots_of, E), ALU.mult))
                settle()
                step(dve.tensor_reduce(end, small[:, 0], AX.X, ALU.add))
                settle()
                step(dve.tensor_tensor(start, end, slots_of, ALU.subtract))
                settle()
                step(dve.scalar_tensor_tensor(out=pos[:, :, :], in0=along(start, NT), scalar=float(SLOT),
                                              in1=pos[:, :, :], op0=ALU.mult, op1=ALU.add))
                settle()
                for n in range(TOPK):
                    step(dve.tensor_tensor(picked[:, n], eq[:, n], pos[:, :, :], ALU.mult))
                settle()
                step(dve.tensor_reduce(rows_f[:, :, :], picked[:, :, :, :], AX.X, ALU.add))
                settle()
                dve.tensor_copy(rows_i[:, :], rows_f.rearrange("p k t -> p (k t)")).then_inc(rows_ready, 1)

            def route_table():
                end = per_e[:, 2]
                step(dve.tensor_tensor(slot_e[:, 0], along(end, TAB), across(iota[:, 0:TAB], E), ALU.is_le))
                settle()
                step(dve.tensor_reduce(slot_f[:, 0], slot_e[:, 0], AX.X, ALU.add))
                settle()
                step(dve.tensor_scalar(slot_f[:, 1], slot_f[:, 0], float(E - 1), None, ALU.min))
                settle()
                step(dve.tensor_scalar(etab[:, :], slot_f[:, 1], float(FF), None, ALU.mult))
                step(dve.tensor_tensor(slot_e[:, 1], along(iota[:, 0:E], TAB), across(slot_f[:, 1], E), ALU.is_equal))
                settle()

            def route_biases(biases, table):
                for j in range(FJ):
                    step(dve.tensor_tensor(slot_e[:, 0], slot_e[:, 1],
                                           along(biases.rearrange("p (e j) -> p j e", j=FJ)[:, j], TAB), ALU.mult))
                    settle()
                    step(dve.tensor_reduce(table[:, j], slot_e[:, 0], AX.X, ALU.add))
                    settle()

            def route_weights():
                dve.wait_ge(gexp_done, 1)
                step(dve.tensor_scalar(rw[:, 2, :], rw[:, 1, :], 1.0, None, ALU.add))
                settle()
                step(dve.reciprocal(rw[:, 3, :], rw[:, 2, :]))
                settle()
                step(dve.tensor_tensor(rw[:, 2, :], rw[:, 1, :], rw[:, 3, :], ALU.mult))
                settle()
                for n in range(TOPK):
                    step(dve.tensor_scalar(wmix[:, n], rw[:, 3 - n, :], IA2, None, ALU.mult))
                    step(dve.tensor_tensor(picked[:, n], eq[:, n], across(rw[:, 3 - n, :], E), ALU.mult))
                settle()
                dve.tensor_tensor(comb[:, :, :], picked[:, 0], picked[:, 1], ALU.add).then_inc(comb_ready, 1)

            def routing(n):
                if n == 4:
                    route_choices()
                elif n == 7:
                    route_rows()
                elif n == 12:
                    route_table()
                elif n == 14:
                    route_biases(w("b1"), b1_t)
                elif n == 16:
                    route_biases(b2_s[:, :], b2_t)
                    dve.sem_inc(table_ready, 1)
                elif n == 18:
                    route_weights()

            def bias(s, k):
                dve.tensor_scalar(b1_e[:, k, :], b1_t[:, :, s], 1.0, None, ALU.mult).then_inc(b1_done, 1)

            def hidden(s, k):
                dve.wait_ge(silu_done, s + 1)
                dve.wait_ge(up_v, s + 1)
                dve.wait_ge(down_ready, s + 1)
                for j in range(FJ):
                    ins = dve.scalar_tensor_tensor(out=hid[:, k, j, :], in0=bank(2 + k, j * SLOT, (j + 1) * SLOT),
                                                   scalar=b2_t[:, j, bass.ds(s, 1)], in1=silu[:, k, j, :],
                                                   op0=ALU.add, op1=ALU.mult)
                ins.then_inc(hid_done, 1)

            def output(s, k):
                dve.wait_ge(down_ready, 2 + s + 1)
                dve.tensor_copy(ys[:, s, :], bank(4 + k, 0, SH * D)).then_inc(y_done, 1)

            def experts():
                dve.sem_inc(y_done, 2)
                for k in range(2):
                    bias(slice(k, k + 1), k)
                for k in range(2):
                    hidden(k, k)
                    bias(slice(k + 2, k + 3), k)
                with dve.Fori(1, SLOTS // 2) as i:
                    for k in range(2):
                        hidden(2 * i + k, k)
                        bias(bass.ds(2 * i + k + 2, 1), k)
                        output(2 * i + k - 2, k)
                for k in range(2):
                    output(SLOTS - 2 + k, k)

            sums = [0]

            def into_acc(ins):
                sums[0] += 1
                ins.then_inc(acc_done, 1)

            def mix(m):
                k, t = m % TOPK, m // TOPK
                dve.wait_ge(gathered[m % YIN], 16 * (m // YIN + 1))
                if sums[0]:
                    dve.wait_ge(acc_done, sums[0])
                into_acc(dve.scalar_tensor_tensor(out=acc[:, t, :], in0=y_in[:, m % YIN, :], scalar=wmix[:, k, t:t + 1],
                                                  in1=acc[:, t, :], op0=ALU.mult, op1=ALU.add))
                dve.sem_inc(mixed, 1)

            def ring_result(item):
                r = ring_at[item]
                kind = item[0]
                b0 = ring_bank(r)
                dve.wait_ge(ring_ready, r + 1)
                if kind == "max1":
                    _, g, j, i = item
                    ins = dve.tensor_reduce(maxima[:, g % 2, j, i:i + 1],
                                            ps[:, b0 * BANK:b0 * BANK + (i + 1) * PART], AX.X, ALU.max)
                elif kind == "max2":
                    _, g, j, i = item
                    pair = ps[:, b0 * BANK:(b0 + 2) * BANK].rearrange("p (k n) -> p k n", k=2)
                    ins = dve.tensor_reduce(maxima[:, g % 2, j:j + 2, i], pair[:, :, 0:(i + 1) * PART], AX.X, ALU.max)
                elif kind == "mT":
                    g = item[1]
                    c = item[2]
                    if g >= 1:
                        dve.wait_ge(mstore[g - 1][c], 16)
                    ins = dve.tensor_copy(max_t[:, c, :], bank(b0, 0, PART // 2, p1=2 * G4 * TPC).bitcast(F16))
                elif kind == "oT":
                    _, g, c = item
                    q = g * CPB + c
                    o = bank(b0).rearrange("p (t j d) -> p t j d", t=TPC, j=G4)
                    step(dve.reciprocal(rden[:, q % 2], o[:, :, :, HD]))
                    settle()
                    h0 = G4 * HD * (g % GPB)
                    dst = attn[:, c * TPC:(c + 1) * TPC, h0:h0 + G4 * HD]
                    ins = dve.tensor_tensor(dst.rearrange("p t (j d) -> p t j d", j=G4), o[:, :, :, 0:HD],
                                            rden[:, q % 2].unsqueeze(3).broadcast_to([PART, TPC, G4, HD]), ALU.mult)
                elif kind == "count":
                    dve.tensor_copy(pos[:, :, :], bank(b0, 0, NT * E).rearrange("p (t e) -> p t e", e=E))
                    ins = dve.tensor_copy(per_e[:, 0], bank(b0 + 1, 0, E))
                else:
                    _, b, c = item
                    tiles = slice(b * KT + c * TPC, b * KT + (c + 1) * TPC)
                    if sums[0]:
                        dve.wait_ge(acc_done, sums[0])
                    ins = dve.tensor_tensor(acc[:, tiles, :], acc[:, tiles, :],
                                            bank(b0).rearrange("p (t d) -> p t d", t=TPC), ALU.add)
                ins.then_inc(ring_done, 1)
                if kind in ("wo", "count"):
                    dve.wait_ge(*taken(r))
                if kind in ("max1", "max2") and item == max_items(item[1], kind == "max1")[-1]:
                    g, c = item[1], int(kind == "max1")
                    dve.wait_ge(*taken(r))
                    m = maxima[:, g % 2, :, c * TPC:(c + 1) * TPC]
                    split = 2 * (CPB * g + c)
                    if g >= 2:
                        dve.wait_ge(ring_ready, ring_at["mT", g - 2, c] + 1)
                    dve.tensor_scalar(max_s[:, g % 2, c, 0], m, -1.0 / KAPPA, None, ALU.mult).then_inc(msplit_done, 1)
                    dve.wait_ge(msplit_done, split + 1)
                    dve.scalar_tensor_tensor(out=max_s[:, g % 2, c, 1], in0=m, scalar=-1.0 / KAPPA,
                                             in1=max_s[:, g % 2, c, 0], op0=ALU.mult, op1=ALU.subtract
                                             ).then_inc(msplit_done, 1)
                    dve.wait_ge(msplit_done, split + 2)

            def ring_results(items):
                for item in items:
                    if not by_act[ring_at[item]]:
                        ring_result(item)

            ring_results(first[:8])
            dve.wait_ge(amax_red, 2)
            powers(3, 5)
            for n, (a, ia) in enumerate(((A1, IA1), (A2, IA2))):
                step(dve.tensor_scalar(a, ipow[:, 3 + n:4 + n], 2.0 ** 13, None, ALU.mult))
                step(dve.tensor_scalar(ia, pow2[:, 3 + n:4 + n], 2.0 ** -13, None, ALU.mult))
            settle()
            dve.sem_inc(scales_ready, 1)
            step(dve.tensor_scalar(b2_s[:, :], w("b2"), A2, None, ALU.mult))
            ring_results(first[8:])
            for n in range(NG * NCOL):
                if n == MID:
                    experts()
                ring_results(slots[n])
                routing(n)
                for m in GATHERS.get(n - 4, ()):
                    mix(m)
            ring_results(tail)


def kernel(**inputs):
    import concourse.bacc as bacc
    from concourse.bass_utils import run_bass_kernel_spmd

    a = {k: np.asarray(v) for k, v in inputs.items()}
    h = DR // 2

    def both(wr):
        return np.concatenate([wr, wr[:, h:], wr[:, :h]], axis=1)

    def by_half(b):
        return b.reshape(E, FJ, PART).transpose(2, 0, 1).reshape(PART, E * FJ)

    f32 = np.float32
    freq = (f32(1.0) / np.power(f32(10000.0), np.arange(0, DR, 2, dtype=f32) / f32(DR))).astype(f32)
    angle = np.outer(np.arange(T, dtype=f32), freq).astype(f32)
    cos, sin = np.cos(angle), np.sin(angle)
    pack = np.concatenate([
        a["L0_attn_W_q"], both(a["L0_attn_W_q_rope"]), a["L0_attn_W_kv_down"], a["L0_attn_W_k_up"],
        both(a["L0_attn_W_k_rope"]), a["L0_attn_W_v_up"], a["L0_attn_W_o"], a["L0_ffn_Wg"].T,
        by_half(a["L0_ffn_b1"]), by_half(a["L0_ffn_b2"]),
        np.broadcast_to(np.arange(32, dtype=f32), (PART, 32))], axis=1)
    arrays = {
        "x": a["L0_attn_x"].reshape(TOK, D),
        "wpack": pack,
        "w12": np.stack([a["L0_ffn_W1"].transpose(2, 0, 1).reshape(D, E * FF),
                         a["L0_ffn_W2"].transpose(2, 0, 1).reshape(D, E * FF)]),
        "w3": a["L0_ffn_W3"].reshape(E, D, FJ, PART).transpose(3, 0, 2, 1).reshape(PART, E * FJ * D),
        "b3": a["L0_ffn_b3"],
        "rope": np.concatenate([cos, cos, -sin, sin], axis=1).reshape(KT, PART, 2 * DR).transpose(1, 0, 2),
        "kappa": np.full((2, T), KAPPA, np.float16),
    }
    arrays = {k: np.ascontiguousarray(v) for k, v in arrays.items()}
    nc = bacc.Bacc("TRN2", target_bir_lowering=False, num_devices=1)
    args = [nc.dram_tensor(k, v.shape, mybir.dt.from_np(v.dtype), kind="ExternalInput").ap()
            for k, v in arrays.items()]
    out = nc.dram_tensor("out", (TOK, D), F32, kind="ExternalOutput").ap()
    build(nc, *args, out)
    r = run_bass_kernel_spmd(nc, [arrays], core_ids=[0])
    return r.results[0]["out"].reshape(B, T, D)
```
